# Optimizing a Trainium2 kernel written in Bass

```python
import numpy as np
import jax
import jax.numpy as jnp

def _softmax(x, axis=-1):
    return jax.nn.softmax(x, axis=axis)
def _gelu(x):
    return jax.nn.gelu(x, approximate=True)
def _silu(x):
    return jax.nn.silu(x)
def _sigmoid(x):
    return jax.nn.sigmoid(x)
def _layernorm(x, axis=-1, eps=1e-5):
    m = jnp.mean(x, axis=axis, keepdims=True)
    v = jnp.var(x, axis=axis, keepdims=True)
    return (x - m) / jnp.sqrt(v + eps)
def _scatter_add(tgt, idx, src, axis=0):
    return tgt.at[idx].add(src)
def _segment_sum(src, seg, n):
    return jax.ops.segment_sum(src, seg, n)

kernel_name = 'mk_conv_attn_hybrid_d2_conv_nhwc128_09f3d7'

def setup_inputs(seed: int = 0):
    np.random.seed(seed)
    _w = jnp.asarray
    def _rec_inputs():
        import jax
        import jax.numpy as jnp
        _gk = jax.random.key(seed)
        x = -0.0005207 + 1.001 * jax.random.normal(jax.random.fold_in(_gk, 1), (4, 64, 64, 128), jnp.float32)
        return x
    x = _rec_inputs()
    def _L0_conv_setup():
        import jax, jax.numpy as jnp
        import numpy as np
        NUM_HEAD = 8

        def conv_same(x, w, b):
            return jax.lax.conv_general_dilated(x, w, window_strides=(1, 1), padding='SAME', dimension_numbers=('NHWC', 'HWIO', 'NHWC')) + b

        def _gated_resnet(x, W1, b1, W2, b2, Wq, bq, Wk, bk, Wv, bv, W3, b3):
            B, H, W, C = x.shape
            c1 = conv_same(jax.nn.elu(x), W1, b1)
            c2 = conv_same(c1, W2, b2)
            a, b = jnp.split(c2, 2, axis=-1)
            c3 = a * jax.nn.sigmoid(b)
            N = H * W
            f = c3.reshape(B, N, C)
            q = f @ Wq + bq
            k = f @ Wk + bk
            v = f @ Wv + bv
            scale = jnp.float32(np.sqrt(C // 8))
            dot = jnp.einsum('bnd,bmd->bnm', q, k) / scale
            mask = jnp.tril(jnp.ones((N, N), jnp.float32), -1)
            dot = dot - (1.0 - mask) * 10000000000.0
            dot = dot - jnp.max(dot, axis=-1, keepdims=True)
            e = jnp.exp(dot) * mask
            probs = e / (jnp.sum(e, axis=-1, keepdims=True) + 1e-10)
            atten = jnp.einsum('bnm,bmd->bnd', probs, v)
            multihead = jnp.tile(atten, (1, 1, NUM_HEAD)).reshape(B, H, W, -1)
            mh = multihead @ W3 + b3
            c3 = c3 + mh.reshape(B, H, W, C)
            return x + c3
        key = jax.random.key(seed)
        ks = jax.random.split(key, 8)
        B, H, W, C = (4, 64, 64, 128)
        DQK, DV = (4, 16)
        s = 0.02
        return {'x': jax.random.normal(ks[0], (B, H, W, C), dtype=jnp.float32), 'W1': jax.random.normal(ks[1], (3, 3, C, C), dtype=jnp.float32) * s, 'b1': jnp.zeros((C,), jnp.float32), 'W2': jax.random.normal(ks[2], (3, 3, C, 2 * C), dtype=jnp.float32) * s, 'b2': jnp.zeros((2 * C,), jnp.float32), 'Wq': jax.random.normal(ks[3], (C, DQK), dtype=jnp.float32) * s, 'bq': jnp.zeros((DQK,), jnp.float32), 'Wk': jax.random.normal(ks[4], (C, DQK), dtype=jnp.float32) * s, 'bk': jnp.zeros((DQK,), jnp.float32), 'Wv': jax.random.normal(ks[5], (C, DV), dtype=jnp.float32) * s, 'bv': jnp.zeros((DV,), jnp.float32), 'W3': jax.random.normal(ks[6], (NUM_HEAD * DV, C), dtype=jnp.float32) * s, 'b3': jnp.zeros((C,), jnp.float32)}
    _L0_conv_all = _L0_conv_setup()
    _L0_conv_in = {k: v for k, v in _L0_conv_all.items() if k in ('W1', 'b1', 'W2', 'b2', 'Wq', 'bq', 'Wk', 'bk', 'Wv', 'bv', 'W3', 'b3', )}
    del _L0_conv_all

    def _L1_attn_setup():
        import jax, jax.numpy as jnp
        import numpy as np
        E = 128
        H = 4
        D = E // H
        key = jax.random.key(seed)
        ks = jax.random.split(key, 5)
        b, n = (4, 4096)
        x = jax.random.normal(ks[0], (b, n, E), dtype=jnp.float32)
        W_qkv = jax.random.normal(ks[1], (E, 3 * E), dtype=jnp.float32) * (1.0 / np.sqrt(E))
        b_qkv = jax.random.normal(ks[2], (3 * E,), dtype=jnp.float32) * 0.01
        W_proj = jax.random.normal(ks[3], (E, E), dtype=jnp.float32) * (1.0 / np.sqrt(E))
        b_proj = jax.random.normal(ks[4], (E,), dtype=jnp.float32) * 0.01
        return {'x': x, 'W_qkv': W_qkv, 'b_qkv': b_qkv, 'W_proj': W_proj, 'b_proj': b_proj}
    _L1_attn_all = _L1_attn_setup()
    _L1_attn_in = {k: v for k, v in _L1_attn_all.items() if k in ('W_qkv', 'b_qkv', 'W_proj', 'b_proj', )}
    del _L1_attn_all

    def _L1_ffn_setup():
        import jax, jax.numpy as jnp
        import numpy as np
        B, N, D, C, E, K = (8, 8192, 128, 128, 8, 2)
        key = jax.random.key(seed)
        k0, k1, k2 = jax.random.split(key, 3)
        x = jax.random.normal(k0, (B, N, D), dtype=jnp.float32)
        router_w = jax.random.normal(k1, (D, E), dtype=jnp.float32) * 0.05
        router_b = jnp.zeros((E,), dtype=jnp.float32)
        expert_w = jax.random.normal(k2, (E, D, C), dtype=jnp.float32) * (1.0 / np.sqrt(D))
        expert_b = jnp.zeros((E, C), dtype=jnp.float32)
        return {'x': x, 'router_w': router_w, 'router_b': router_b, 'expert_w': expert_w, 'expert_b': expert_b}
    _L1_ffn_all = _L1_ffn_setup()
    _L1_ffn_in = {k: v for k, v in _L1_ffn_all.items() if k in ('router_w', 'router_b', 'expert_w', 'expert_b', )}
    del _L1_ffn_all

    return {
        "x": x,
        "L0_conv_W1": _L0_conv_in["W1"],
        "L0_conv_b1": _L0_conv_in["b1"],
        "L0_conv_W2": _L0_conv_in["W2"],
        "L0_conv_b2": _L0_conv_in["b2"],
        "L0_conv_Wq": _L0_conv_in["Wq"],
        "L0_conv_bq": _L0_conv_in["bq"],
        "L0_conv_Wk": _L0_conv_in["Wk"],
        "L0_conv_bk": _L0_conv_in["bk"],
        "L0_conv_Wv": _L0_conv_in["Wv"],
        "L0_conv_bv": _L0_conv_in["bv"],
        "L0_conv_W3": _L0_conv_in["W3"],
        "L0_conv_b3": _L0_conv_in["b3"],
        "L1_attn_W_qkv": _L1_attn_in["W_qkv"],
        "L1_attn_b_qkv": _L1_attn_in["b_qkv"],
        "L1_attn_W_proj": _L1_attn_in["W_proj"],
        "L1_attn_b_proj": _L1_attn_in["b_proj"],
        "L1_ffn_router_w": _L1_ffn_in["router_w"],
        "L1_ffn_router_b": _L1_ffn_in["router_b"],
        "L1_ffn_expert_w": _L1_ffn_in["expert_w"],
        "L1_ffn_expert_b": _L1_ffn_in["expert_b"],
    }

def reference(x, L0_conv_W1, L0_conv_b1, L0_conv_W2, L0_conv_b2, L0_conv_Wq, L0_conv_bq, L0_conv_Wk, L0_conv_bk, L0_conv_Wv, L0_conv_bv, L0_conv_W3, L0_conv_b3, L1_attn_W_qkv, L1_attn_b_qkv, L1_attn_W_proj, L1_attn_b_proj, L1_ffn_router_w, L1_ffn_router_b, L1_ffn_expert_w, L1_ffn_expert_b):
    import jax
    import jax.numpy as jnp
    def _L0_conv_ref(x, W1, b1, W2, b2, Wq, bq, Wk, bk, Wv, bv, W3, b3):
        import jax, jax.numpy as jnp
        import numpy as np
        NUM_HEAD = 8

        def conv_same(x, w, b):
            return jax.lax.conv_general_dilated(x, w, window_strides=(1, 1), padding='SAME', dimension_numbers=('NHWC', 'HWIO', 'NHWC')) + b

        def _gated_resnet(x, W1, b1, W2, b2, Wq, bq, Wk, bk, Wv, bv, W3, b3):
            B, H, W, C = x.shape
            c1 = conv_same(jax.nn.elu(x), W1, b1)
            c2 = conv_same(c1, W2, b2)
            a, b = jnp.split(c2, 2, axis=-1)
            c3 = a * jax.nn.sigmoid(b)
            N = H * W
            f = c3.reshape(B, N, C)
            q = f @ Wq + bq
            k = f @ Wk + bk
            v = f @ Wv + bv
            scale = jnp.float32(np.sqrt(C // 8))
            dot = jnp.einsum('bnd,bmd->bnm', q, k) / scale
            mask = jnp.tril(jnp.ones((N, N), jnp.float32), -1)
            dot = dot - (1.0 - mask) * 10000000000.0
            dot = dot - jnp.max(dot, axis=-1, keepdims=True)
            e = jnp.exp(dot) * mask
            probs = e / (jnp.sum(e, axis=-1, keepdims=True) + 1e-10)
            atten = jnp.einsum('bnm,bmd->bnd', probs, v)
            multihead = jnp.tile(atten, (1, 1, NUM_HEAD)).reshape(B, H, W, -1)
            mh = multihead @ W3 + b3
            c3 = c3 + mh.reshape(B, H, W, C)
            return x + c3
        return _gated_resnet(x, W1, b1, W2, b2, Wq, bq, Wk, bk, Wv, bv, W3, b3)

    def _L1_attn_ref(x, W_qkv, b_qkv, W_proj, b_proj):
        import jax, jax.numpy as jnp
        import numpy as np
        E = 128
        H = 4
        D = E // H
        b, n, e = x.shape
        qkv = (x @ W_qkv + b_qkv).reshape(b, n, H, D, 3)
        qkv = jnp.transpose(qkv, (4, 0, 2, 1, 3))
        q, k, v = (qkv[0], qkv[1], qkv[2])
        scale = 1.0 / np.float32(np.sqrt(e))
        scores = jnp.einsum('bhnd,bhmd->bhnm', q, k) * scale
        att = jax.nn.softmax(scores, axis=-1)
        out = jnp.einsum('bhnm,bhmd->bhnd', att, v)
        out = jnp.transpose(out, (0, 2, 1, 3)).reshape(b, n, e)
        return out @ W_proj + b_proj

    def _L1_ffn_ref(x, router_w, router_b, expert_w, expert_b):
        import jax, jax.numpy as jnp
        import numpy as np
        B, N, D, C, E, K = (8, 8192, 128, 128, 8, 2)
        router_probs = jax.nn.softmax(x @ router_w + router_b, axis=-1)
        top_p, top_i = jax.lax.top_k(router_probs, K)
        top_p = top_p / jnp.sum(top_p, axis=-1, keepdims=True)
        expert_out = jnp.einsum('bnd,edc->bnec', x, expert_w) + expert_b
        gathered = jnp.take_along_axis(expert_out, top_i[..., None], axis=2)
        return jnp.einsum('bnk,bnkc->bnc', top_p, gathered)

    def _gn(v, G=32, eps=1e-5):
        B_, H_, W_, C_ = v.shape
        g = v.reshape(B_, H_, W_, G, C_ // G)
        m = jnp.mean(g, axis=(1, 2, 4), keepdims=True)
        s = jnp.var(g, axis=(1, 2, 4), keepdims=True)
        return ((g - m) / jnp.sqrt(s + eps)).reshape(v.shape)

    def _ln_c(v, eps=1e-6):
        m = jnp.mean(v, axis=-1, keepdims=True)
        s = jnp.var(v, axis=-1, keepdims=True)
        return (v - m) / jnp.sqrt(s + eps)

    def _ln_t(v, eps=1e-5):
        m = jnp.mean(v, axis=-1, keepdims=True)
        s = jnp.var(v, axis=-1, keepdims=True)
        return (v - m) / jnp.sqrt(s + eps)

    def _to_tokens(v):
        B_, H_, W_, C_ = v.shape
        return v.reshape(B_, H_ * W_, C_)
    def _from_tokens(t, like):
        return t.reshape(like.shape)

    x = _L0_conv_ref(x, L0_conv_W1, L0_conv_b1, L0_conv_W2, L0_conv_b2, L0_conv_Wq, L0_conv_bq, L0_conv_Wk, L0_conv_bk, L0_conv_Wv, L0_conv_bv, L0_conv_W3, L0_conv_b3)
    t = _to_tokens(x)
    t = t + _L1_attn_ref(_ln_t(t), L1_attn_W_qkv, L1_attn_b_qkv, L1_attn_W_proj, L1_attn_b_proj)
    t = t + _L1_ffn_ref(_ln_t(t), L1_ffn_router_w, L1_ffn_router_b, L1_ffn_expert_w, L1_ffn_expert_b)
    x = _from_tokens(t, x)
    return x


_drawn_inputs = setup_inputs


def setup_inputs(seed=0):
    import zlib

    import numpy as np

    out = dict(_drawn_inputs(seed))
    spreads = {'L0_conv_b1': (0.0, 0.1),
     'L0_conv_b2': (0.0, 0.1),
     'L0_conv_bq': (0.0, 2.0),
     'L0_conv_bk': (0.0, 2.0),
     'L0_conv_bv': (0.0, 0.1),
     'L0_conv_b3': (0.0, 0.1),
     'L1_ffn_router_b': (0.0, 0.1),
     'L1_ffn_expert_b': (0.0, 0.1)}
    factors = {'L0_conv_Wq': 64.0, 'L0_conv_Wk': 55.28}
    for name, (base, spread) in spreads.items():
        noise = np.random.default_rng([zlib.crc32(name.encode()), seed]).standard_normal(out[name].shape)
        drawn = base * np.exp(spread * noise) if base else spread * noise
        out[name] = jnp.asarray(drawn.astype(out[name].dtype))
    for name, factor in factors.items():
        out[name] = (out[name] * factor).astype(out[name].dtype)
    return out
```

```python
from contextlib import ExitStack

import concourse.bass as bass
from concourse import mybir

ALU = mybir.AluOpType
ACT = mybir.ActivationFunctionType
F32 = mybir.dt.float32
F32R = mybir.dt.float32r
I32 = mybir.dt.int32
AX_X = mybir.AxisListType.X

P = 128
IMG = 64
PAD = IMG + 2
N = IMG * IMG
B = 4
T = N // P
CH = 512
J = N // CH
CT = CH // P
ROWS = CH // IMG
H, D = 4, 32
DQK, DV = 4, 16
E = 8
RING = 4
GROUP = 4
SAFE = 60.0

C_ID, C_TRI, C_TRI0, C_DEN, C_MASK, C_HEAD, C_DESC, C_COLS = 0, 128, 640, 768, 896, 898, 902, 910


def constants():
    import numpy as np
    c = np.zeros((P, C_COLS), np.float32)
    p = np.arange(P)
    c[:, C_ID:C_ID + P] = np.eye(P)
    tri = np.where(p[None, :] < p[:, None], 0.0, -4.0e10)
    c[:, C_TRI + CH - P:C_TRI + CH] = tri
    c[:, C_TRI0:C_TRI0 + P] = tri
    c[0, C_TRI0] = 0.0
    c[DV::32, C_DEN:C_DEN + P] = 1.0
    c[0:16, C_MASK] = [(r // DQK) % 2 for r in range(16)]
    c[0:16, C_MASK + 1] = [r // (2 * DQK) for r in range(16)]
    c[p, C_HEAD + p // D] = 1.0
    c[:, C_DESC:C_DESC + E] = np.arange(E, 0, -1)
    return c


PAIRS0 = sum(2 * (j + 1) for j in range(J))
TILES0 = sum(CT * (j + 1) for j in range(J))
QUADS0 = PAIRS0 // 2
STEPS = 79
LOOPS = J // 2
F_STEPS = J * (1 + CT * 9)
L_STEPS = 2
ENGINES = 5


def conv_hybrid_kernel(nc, a, consts, out):
    with ExitStack() as ctx:
        def sb(name, shape, dt=F32):
            return ctx.enter_context(nc.sbuf_tensor(name, shape, dt))

        def sem(name):
            return ctx.enter_context(nc.semaphore(name))

        ps = ctx.enter_context(nc.psum_tensor("ps", [P, 8, CH], F32))

        con = sb("con", [P, C_COLS])
        b1 = sb("b1", [P, 1])
        b2 = sb("b2", [P, 2])
        b2h = sb("b2h", [P, 1])
        wq0 = sb("wq0", [P, 16])
        wk0 = sb("wk0", [P, 16])
        wv0 = sb("wv0", [P, DV])
        bqk0 = sb("bqk0", [16, 2])
        bqk0m = sb("bqk0m", [16, 2])
        bv0 = sb("bv0", [P, DV])
        w3 = sb("w3", [P, P])
        b3 = sb("b3", [P, 1])
        wqkv = sb("wqkv", [P, 3 * P])
        bqkv = sb("bqkv", [P, 3])
        bqkv_abs = sb("bqkv_abs", [P, 3])
        bqkv_row = sb("bqkv_row", [P, 3 * P])
        wproj = sb("wproj", [P, P])
        bproj = sb("bproj", [P, P])
        rw = sb("rw", [P, E])
        rb = sb("rb", [P, E])
        ew = sb("ew", [P, E, P])
        eb = sb("eb", [P, CT, P])
        ones32 = sb("ones32", [P, 32])

        xt = sb("xt", [P, T, P])
        prob = sb("prob", [P, RING, H, CH])
        psum4 = sb("psum4", [P, H, CH])
        w3all = psum4[:, 0:2, :].rearrange("p a b -> p (a b)").rearrange("p (h c) -> p h c", c=P)
        work = sb("work", [P, 4, CH])
        mv = sb("mv", [P, T, 2])
        stats = sb("stats", [P, T, 6])
        rstd = sb("rstd", [P, T])
        nmr = sb("nmr", [P, T])
        mx = sb("mx", [P, CT, J])
        mneg = sb("mneg", [P, H, CT])
        absq = sb("absq", [P, J])
        absk = sb("absk", [P, J])
        bound = sb("bound", [P, 4])
        flag = sb("flag", [1, 8])
        xhT = sb("xhT", [P, (J + 1) * CH])
        early = ExitStack()

        def sbe(name, shape, dt=F32):
            return early.enter_context(nc.sbuf_tensor(name, shape, dt))

        w1 = sbe("w1", [P, 9, P])
        w2 = sbe("w2", [P, 9, 2 * P])
        c0 = sbe("c0", [P, PAD, PAD])
        c1 = sbe("c1", [P, PAD, PAD])
        c3 = sbe("c3", [P, J, CH])
        q0 = sbe("q0", [33, J, CH], F32R)
        k0 = sbe("k0", [33, J, CH], F32R)
        v0 = sbe("v0", [P, T, 32])
        early.close()
        kst = sb("kst", [P, H, N], F32R)
        qst = sb("qst", [P, 2, H, CH], F32R)
        hi = sb("hi", [P, 2, CH], F32R)
        lo = sb("lo", [P, 2, CH], F32R)
        v1 = sb("v1", [P, T, P])

        ident = con[:, C_ID:C_ID + P]

        s_w = sem("weights_loaded")
        s_zero = sem("rows_zeroed")
        s_prep = sem("weights_ready")
        s_batch = sem("batch_done")
        s_none = sem("unused")
        s_x = [sem(f"x_loaded{q}") for q in range(4)]
        s_cw = [sem(f"conv_weights_loaded{q}") for q in range(2)]
        s_border = sem("borders_zero")
        s_xT = sem("x_transposed")
        s_min = sem("min_done")
        s_eexp = sem("elu_exp_done")
        s_elu = sem("elu_done")
        s_conv1 = sem("conv1_summed")
        s_c1 = sem("conv1_stored")
        s_conv2 = sem("conv2_summed")
        s_tanh = sem("tanh_done")
        s_c3 = sem("gated_done")
        s_qk0 = sem("qk0_multiplied")
        s_hm0 = sem("qk0_high_parts")
        s_qk0s = sem("qk0_stacked")
        s_v0m = sem("v0_multiplied")
        s_v0 = sem("v0_stored")
        s_ms = sem("max_scores")
        s_mu = sem("max_taken")
        s_mneg = sem("shift0_done")
        s_mrow = sem("shift0_row")
        s_mput = sem("shift0_stored")
        s_s0 = sem("scores0")
        s_e0 = sem("exp0_done")
        s_mask0 = sem("exp0_masked")
        s_pv0 = sem("pv0_done")
        s_acc0 = sem("acc0_copied")
        s_fin0 = sem("mh0_multiplied")
        s_t0 = sem("t0_transposed_ready")
        s_t0T = sem("t0_transposed")
        s_t0s = sem("t0_stored")
        s_var = sem("variance_ready")
        s_sqrt = sem("sqrt_done")
        s_xh = sem("normalised")
        s_xhT = sem("normalised_transposed")
        s_xhs = sem("normalised_stored")
        s_qkv1 = sem("qkv1_multiplied")
        s_absk = sem("k1_bound_taken")
        s_khi = sem("k1_high_done")
        s_klo = sem("k1_low_done")
        s_v1 = sem("v1_stored")
        s_kst = [sem(f"k_stacked{q}") for q in range(2)]
        s_bm = sem("bound_multiplied")
        s_bnd = sem("bound_ready")
        s_flag = sem("flag_ready")
        s_bp = sem("proj_bias_added")
        s_qp = sem("q1_multiplied")
        s_qhi = sem("q1_high_done")
        s_qlo = sem("q1_low_done")
        s_qst = [sem(f"q_stacked{q}") for q in range(2)]
        s_gs = sem("general_scores")
        s_gu = sem("general_max_taken")
        s_gm = sem("general_shift_done")
        s_gr = sem("general_shift_row")
        s_shift = sem("shift_stored")
        s_s1 = sem("scores1")
        s_e1 = sem("exp1_done")
        s_pv1 = sem("pv1_done")
        s_sum = sem("group_sums")
        s_dg = sem("group_sums_used")
        s_o1 = sem("attention_out")
        s_pr = sem("projected")
        s_t1 = sem("t1_stored")
        s_rl = sem("router_multiplied")
        s_rexpi = sem("router_exp_ready")
        s_rexp = sem("router_exp_done")
        s_g = sem("gates_ready")
        s_gT = sem("gates_transposed")
        s_gTs = sem("gates_stored")
        s_eb = sem("expert_bias_multiplied")
        s_y = sem("expert_multiplied")
        s_yu = sem("expert_used")
        s_r = sem("result_ready")
        s_out = [sem(f"stored{q}") for q in range(2)]
        s_v = sem("vector_steps")
        s_vl = sem("vector_loop_steps")
        s_vf = sem("vector_combine_steps")

        x_tok = a["x"].rearrange("b h w c -> b (h w) c").rearrange("b (t p) c -> b p t c", p=P)
        out_tok = out.rearrange("b h w c -> b (h w) c").rearrange("b (t p) c -> b p t c", p=P)

        weight_loads = [
            (con[:, :], consts),
            (b1[:, :], a["L0_conv_b1"].rearrange("(c o) -> c o", o=1)),
            (b2[:, 0:1], a["L0_conv_b2"][0:P].rearrange("(c o) -> c o", o=1)),
            (b2[:, 1:2], a["L0_conv_b2"][P:2 * P].rearrange("(c o) -> c o", o=1)),
            (wv0[:, :], a["L0_conv_Wv"]),
            (bv0[:, :], a["L0_conv_bv"].partition_broadcast(P)),
            (b3[:, :], a["L0_conv_b3"].rearrange("(c o) -> c o", o=1)),
            (wqkv[:, :], a["L1_attn_W_qkv"]),
            (bqkv[:, :], a["L1_attn_b_qkv"].rearrange("(c s) -> c s", s=3)),
            (bqkv_row[:, :], a["L1_attn_b_qkv"].partition_broadcast(P)),
            (wproj[:, :], a["L1_attn_W_proj"]),
            (bproj[:, :], a["L1_attn_b_proj"].partition_broadcast(P)),
            (rw[:, :], a["L1_ffn_router_w"]),
            (rb[:, :], a["L1_ffn_router_b"].partition_broadcast(P)),
            (ew[:, :, :], a["L1_ffn_expert_w"].rearrange("e d c -> d e c")),
        ]
        for g in range(4):
            weight_loads += [
                (wq0[:, DQK * g:DQK * g + DQK], a["L0_conv_Wq"]),
                (wk0[:, DQK * g:DQK * g + DQK], a["L0_conv_Wk"]),
                (bqk0[DQK * g:DQK * g + DQK, 0:1], a["L0_conv_bq"].rearrange("(c o) -> c o", o=1)),
                (bqk0[DQK * g:DQK * g + DQK, 1:2], a["L0_conv_bk"].rearrange("(c o) -> c o", o=1)),
                (w3all[32 * g:32 * g + DV, :, :], a["L0_conv_W3"].rearrange("(h d) c -> d h c", d=DV)),
                (eb[32 * g:32 * g + E, g, :], a["L1_ffn_expert_b"]),
            ]
        PREP = 3

        def ws(s):
            return wqkv[:, :].rearrange("p (c s) -> p s c", s=3)[:, s, :]

        def inner(padded, j, dy=1, dx=1):
            return padded[:, ROWS * j + dy:ROWS * j + dy + ROWS, dx:dx + IMG]

        def rows(ap):
            return ap.rearrange("p (r w) -> p r w", w=IMG)

        def pair_of(j, i):
            return j * (j + 1) + i

        block = ctx.enter_context(nc.Block())

        @block.sync
        def _(sp):
            sp.wait_ge(s_zero, 2)
            for dst, src in weight_loads:
                sp.dma_start(dst, src).then_inc(s_w, 16)
            sp.sem_inc(s_batch, 1)
            with sp.Fori(0, B) as b:
                sp.wait_ge(s_batch, b * ENGINES + ENGINES)
                for q in range(4):
                    sp.dma_start(xt[:, 8 * q:8 * q + 8, :], x_tok[b][:, 8 * q:8 * q + 8, :]).then_inc(s_x[q], 16)
                sp.dma_start(w1[:, :, :], a["L0_conv_W1"].rearrange("kh kw i o -> i (kh kw) o")).then_inc(s_cw[0], 16)
                sp.dma_start(w2[:, :, :], a["L0_conv_W2"].rearrange("kh kw i o -> i (kh kw) o")).then_inc(s_cw[1], 16)
                for j in range(J):
                    sp.wait_ge(s_klo, b * J + j + 1)
                    for h in range(H):
                        for g, part in enumerate((hi, hi, lo)):
                            sp.dma_start(kst[32 * g:32 * g + D, h, CH * j:CH * j + CH].bitcast(F32),
                                         part[D * h:D * h + D, j % 2, :].bitcast(F32)).then_inc(s_kst[j % 2], 16)
                sp.wait_ge(s_qlo, b * (J + 1) + 1)
                for h in range(H):
                    for g, part in enumerate((hi, lo, hi)):
                        sp.dma_start(qst[32 * g:32 * g + D, 0, h, :].bitcast(F32),
                                     part[D * h:D * h + D, 0, :].bitcast(F32)).then_inc(s_qst[0], 16)
                with sp.Fori(0, LOOPS) as i:
                    for u in range(2):
                        sp.wait_ge(s_qlo, b * (J + 1) + i * 2 + (u + 2))
                        for h in range(H):
                            for g, part in enumerate((hi, lo, hi)):
                                sp.dma_start(qst[32 * g:32 * g + D, 1 - u, h, :].bitcast(F32),
                                             part[D * h:D * h + D, 1 - u, :].bitcast(F32)).then_inc(s_qst[1 - u], 16)
                for j in range(J):
                    sp.wait_ge(s_r, b * J + j + 1)
                    sp.dma_start(out_tok[b][:, CT * j:CT * j + CT, :],
                                 work[:, 2 + j % 2, :].rearrange("p (t c) -> p t c", c=P)).then_inc(s_out[j % 2], 16)
                for q in range(2):
                    sp.wait_ge(s_out[q], b * (8 * J) + 8 * J)
                sp.sem_inc(s_batch, 1)
            for q in range(2):
                sp.wait_ge(s_out[q], B * 8 * J)

        @block.gpsimd
        def _(pool):
            pool.memset(w3all[:, :, :], 0.0).then_inc(s_zero, 1)
            pool.memset(eb[:, :, :], 0.0).then_inc(s_zero, 1)
            pool.sem_inc(s_batch, 1)
            with pool.Fori(0, B) as b:
                pool.wait_ge(s_batch, b * ENGINES + ENGINES)
                pool.sem_inc(s_none, 1)
                for c in (c0, c1):
                    pool.memset(c[:, 0, :], 0.0)
                    pool.memset(c[:, PAD - 1, :], 0.0)
                    pool.memset(c[:, 1:PAD - 1, 0:1], 0.0)
                    pool.memset(c[:, 1:PAD - 1, PAD - 1:PAD], 0.0).then_inc(s_border, 1)
                pool.memset(q0[:, :, :].bitcast(F32), 0.0).then_inc(s_border, 1)
                pool.memset(k0[:, :, :].bitcast(F32), 0.0).then_inc(s_border, 1)
                pool.memset(v0[:, :, DV + 1:32], 0.0)
                pool.memset(v0[:, :, DV:DV + 1], 1.0).then_inc(s_border, 1)
                pool.wait_ge(s_border, b * 7 + 5)
                pool.sem_inc(s_none, 1)
                pool.memset(k0[32:33, :, :].bitcast(F32), 1.0).then_inc(s_border, 1)
                pool.wait_ge(s_border, b * 7 + 6)
                pool.sem_inc(s_border, 1)
                for j in range(J):
                    for i in range(CT):
                        n = pair_of(j, 2 * j + i // 2)
                        pool.wait_ge(s_e0, b * PAIRS0 + n + 1)
                        pool.sem_inc(s_none, 1)
                        tile = prob[:, n % RING, i % 2, 0:(i + 1) * P]
                        pool.affine_select(out=tile, in_=tile, pattern=[[1, (i + 1) * P]],
                                           compare_op=ALU.is_gt, fill=0.0, base=-P * i,
                                           channel_multiplier=-1).then_inc(s_mask0, 1)
                pool.wait_ge(s_xh, b * (2 * J) + J)
                pool.wait_ge(s_t0s, b * J + J)
                pool.sem_inc(s_none, 1)
                pool.memset(kst[96:97, :, :].bitcast(F32), 1.0).then_inc(s_bp, 1)
                pool.wait_ge(s_bp, b * 2 + 1)
                pool.sem_inc(s_none, 1)
                pool.tensor_tensor(xt[:, :, :], xt[:, :, :],
                                   bproj[:, :].unsqueeze(1).broadcast_to([P, T, P]), ALU.add).then_inc(s_bp, 1)
                pool.wait_ge(s_bp, b * 2 + 2)
                pool.sem_inc(s_batch, 1)

        @block.scalar
        def _(act):
            act.wait_ge(s_prep, PREP)
            act.sem_inc(s_e1, 2)
            act.sem_inc(s_batch, 1)
            with act.Fori(0, B) as b:
                act.wait_ge(s_batch, b * ENGINES + ENGINES)
                act.sem_inc(s_none, 1)
                for j in range(J):
                    act.wait_ge(s_min, b * J + j + 1)
                    act.activation(work[:, 2 + j % 2, :], work[:, j % 2, :], ACT.Exp).then_inc(s_eexp, 1)
                for j in range(J):
                    act.wait_ge(s_conv1, b * J + j + 1)
                    if j == 0:
                        act.wait_ge(s_border, b * 7 + 2)
                    act.activation(inner(c1, j), rows(ps[:, 2 + j % 2, :]), ACT.Identity,
                                   bias=b1[:, 0:1]).then_inc(s_c1, 1)
                for j in range(J):
                    act.wait_ge(s_conv2, b * J + j + 1)
                    if j >= 2:
                        act.wait_ge(s_c3, b * J + j - 1)
                    act.activation(work[:, j % 2, :], ps[:, 6 + j % 2, :], ACT.Tanh, scale=0.5,
                                   bias=b2h[:, 0:1]).then_inc(s_tanh, 1)
                for j in range(J):
                    act.wait_ge(s_qk0, b * J + j + 1)
                    if j:
                        act.wait_ge(s_qk0s, b * J + j)
                    for s in range(2):
                        last = act.activation(work[0:16, 2 + s, :].bitcast(F32R), ps[0:16, s, :], ACT.Identity,
                                              bias=bqk0m[:, s:s + 1], scale=con[0:16, C_MASK + s:C_MASK + s + 1])
                    last.then_inc(s_hm0, 1)
                for j in range(J):
                    for i in range(2 * (j + 1)):
                        n = pair_of(j, i)
                        act.wait_ge(s_s0, b * PAIRS0 + n + 1)
                        if n >= RING:
                            act.wait_ge(s_pv0, b * QUADS0 + (n - RING) // 2 + 1)
                        bank = 2 + 2 * (n % 2)
                        act.activation(prob[:, n % RING, 0:2, :], ps[:, bank:bank + 2, :], ACT.Exp,
                                       scale=0.25).then_inc(s_e0, 1)
                    act.wait_ge(s_pv0, b * QUADS0 + pair_of(j, 2 * (j + 1)) // 2)
                    if j:
                        act.wait_ge(s_fin0, b * J + j)
                    act.activation(work[:, 0, :], ps[:, 6, :], ACT.Copy).then_inc(s_acc0, 1)

                def norm(k):
                    act.wait_ge(s_var, b * 2 + k + 1)
                    act.activation(rstd[:, :], rstd[:, :], ACT.Sqrt).then_inc(s_sqrt, 1)
                    for j in range(J):
                        act.wait_ge(s_xhT, b * (2 * J) + k * J + j + 1)
                        last = act.activation(xhT[:, CH * j:CH * j + CH], ps[:, j % 2, :], ACT.Copy)
                        if j == 0 and k == 0:
                            last = act.activation(xhT[:, N:N + CH], ps[:, 0, :], ACT.Copy)
                        last.then_inc(s_xhs, 1)

                act.wait_ge(s_t0s, b * J + J)
                norm(0)
                for j in range(J):
                    act.wait_ge(s_absk, b * J + j + 1)
                    if j >= 2:
                        act.wait_ge(s_kst[j % 2], b * (12 * 16 * J // 2) + 12 * 16 * (j // 2))
                    act.activation(hi[:, j % 2, :], ps[:, 3, :], ACT.Identity, bias=bqkv[:, 1:2]).then_inc(s_khi, 1)

                def q_high(u, count):
                    act.wait_ge(s_qp, count)
                    act.sem_inc(s_none, 1)
                    act.activation(hi[:, u, :], ps[:, 4 + 2 * u, :], ACT.Identity, bias=bqkv[:, 0:1]).then_inc(s_qhi, 1)

                for q in range(2):
                    act.wait_ge(s_kst[q], b * (12 * 16 * J // 2) + 12 * 16 * J // 2)
                q_high(0, b * (J + 1) + 1)
                with act.Fori(0, LOOPS) as i:
                    g = b * LOOPS + i
                    for u in range(2):
                        for kt in range(T):
                            n = T * u + kt
                            act.wait_ge(s_pv1, g * (2 * T) + n + 1)
                            act.wait_ge(s_sum, g * (2 * T // GROUP * 3) + 3 * (n // GROUP) + (1, 1, 2, 3)[n % GROUP])
                            for h2 in range(2):
                                act.wait_ge(s_s1, g * (4 * T) + 2 * n + h2 + 1)
                                act.activation(prob[:, n % RING, 2 * h2:2 * h2 + 2, :], ps[:, 2 * h2:2 * h2 + 2, :],
                                               ACT.Exp, scale=float(P) ** -0.5).then_inc(s_e1, 1)
                            if kt == 12:
                                q_high(1 - u, b * (J + 1) + i * 2 + (u + 2))
                act.wait_ge(s_t1, b * J + J)
                norm(1)
                act.wait_ge(s_rexpi, b + 1)
                act.sem_inc(s_none, 1)
                act.activation(work[:, 0, 0:T * E], work[:, 0, 0:T * E], ACT.Exp).then_inc(s_rexp, 1)
                act.wait_ge(s_gT, b + 1)
                act.activation(work[:, 1, :], ps[:, 3, :], ACT.Copy)
                act.activation(psum4[:, 0, :], ps[:, 4, :], ACT.Copy).then_inc(s_gTs, 1)
                act.wait_ge(s_gTs, b + 1)
                act.sem_inc(s_batch, 1)

        @block.vector
        def _(dve):
            steps = [0]

            def step(ins, base):
                steps[0] += 1
                ins.then_inc(s_v, 1)
                dve.wait_ge(s_v, base + steps[0])

            dve.memset(ones32[:, :], 1.0).then_inc(s_prep, 1)
            dve.wait_ge(s_w, 16 * len(weight_loads))
            dve.tensor_reduce(w3[:, :], w3all[:, :, :].rearrange("p h c -> p c h"), AX_X, ALU.add)
            dve.tensor_scalar(b2h[:, :], b2[:, 1:2], 0.5, None, ALU.mult)
            dve.scalar_tensor_tensor(bqkv_abs[:, :], bqkv[:, :], -1.0, bqkv[:, :], ALU.mult, ALU.max).then_inc(s_prep, 1)
            dve.tensor_tensor(bqk0m[:, :], bqk0[:, :], con[0:16, C_MASK:C_MASK + 2], ALU.mult).then_inc(s_prep, 1)
            dve.wait_ge(s_prep, PREP)
            dve.sem_inc(s_sum, 3)
            dve.sem_inc(s_batch, 1)
            with dve.Fori(0, B) as b:
                vb = b * STEPS
                dve.wait_ge(s_batch, b * ENGINES + ENGINES)
                dve.sem_inc(s_none, 1)

                def elu_min(j):
                    dve.wait_ge(s_xT, b * J + j + 1)
                    dve.tensor_scalar(work[:, j % 2, :], ps[:, j % 2, :], 0.0, None, ALU.min).then_inc(s_min, 1)

                dve.wait_ge(s_border, b * 7 + 1)
                elu_min(0)
                for j in range(J):
                    if j + 1 < J:
                        elu_min(j + 1)
                    dve.wait_ge(s_eexp, b * J + j + 1)
                    dve.scalar_tensor_tensor(inner(c0, j), rows(work[:, 2 + j % 2, :]), -1.0,
                                             rows(ps[:, j % 2, :]), ALU.add, ALU.max).then_inc(s_elu, 1)
                for j in range(J):
                    dve.wait_ge(s_tanh, b * J + j + 1)
                    gate = work[:, j % 2, :]
                    step(dve.tensor_scalar(gate, gate, 0.5, 0.5, ALU.mult, ALU.add), vb)
                    dve.scalar_tensor_tensor(c3[:, j, :], ps[:, 4 + j % 2, :], b2[:, 0:1], gate,
                                             ALU.add, ALU.mult).then_inc(s_c3, 1)
                dve.wait_ge(s_border, b * 7 + 7)
                for j in range(J):
                    dve.wait_ge(s_hm0, b * J + j + 1)
                    for s, dst in enumerate((q0, k0)):
                        last = dve.scalar_tensor_tensor(dst[0:16, j, :], ps[0:16, s, :], bqk0[:, s:s + 1],
                                                        work[0:16, 2 + s, :], ALU.add, ALU.subtract)
                    last.then_inc(s_qk0s, 1)
                    dve.wait_ge(s_v0m, b * J + j + 1)
                    dve.tensor_tensor(v0[:, CT * j:CT * j + CT, 0:DV],
                                      ps[:, 4 + j % 2, 0:CT * DV].rearrange("p (t d) -> p t d", d=DV),
                                      bv0[:, :].unsqueeze(1).broadcast_to([P, CT, DV]), ALU.add).then_inc(s_v0, 1)

                tile_no = [0]

                def max_tiles(j):
                    for qt in range(CT):
                        for c in range(j + 1):
                            m = tile_no[0]
                            tile_no[0] += 1
                            dve.wait_ge(s_ms, b * TILES0 + m + 1)
                            if c < j:
                                ins = dve.tensor_reduce(mx[:, qt, c:c + 1], ps[:, m % 2, :], AX_X, ALU.max)
                            else:
                                dve.sem_inc(s_none, 1)
                                w = (qt + 1) * P
                                mask = con[:, C_TRI0:C_TRI0 + P] if j == qt == 0 else con[:, C_TRI + CH - w:C_TRI + CH]
                                ins = dve.tensor_tensor_reduce(out=ps[:, m % 2, 0:w], in0=ps[:, m % 2, 0:w], in1=mask,
                                                               scale=1.0, scalar=-3.0e38, op0=ALU.add, op1=ALU.max,
                                                               accum_out=mx[:, qt, c:c + 1])
                            ins.then_inc(s_mu, 1)
                    dve.wait_ge(s_mu, b * TILES0 + tile_no[0])
                    dve.tensor_reduce(mneg[:, 0, :], mx[:, :, 0:j + 1], AX_X, ALU.max, negate=True).then_inc(s_mneg, 1)
                    dve.wait_ge(s_mrow, b * J + j + 1)
                    dve.tensor_copy(q0[32:33, j, :], ps[32:33, 7, :]).then_inc(s_mput, 1)

                def finish0(j):
                    dve.wait_ge(s_fin0, b * J + j + 1)
                    rden, mh = work[:, 2, :], work[:, 3, :]
                    step(dve.tensor_scalar(rden, ps[:, 1, :], 1e-10, None, ALU.add), vb)
                    step(dve.reciprocal(rden, rden), vb)
                    step(dve.tensor_tensor(mh, ps[:, 0, :], rden, ALU.mult), vb)
                    dve.scalar_tensor_tensor(mh, mh, b3[:, 0:1], c3[:, j, :], ALU.add, ALU.add).then_inc(s_t0, 1)
                    dve.wait_ge(s_t0T, b * J + j + 1)
                    t = xt[:, CT * j:CT * j + CT, :]
                    dve.tensor_tensor(t, t, ps[:, 7, :].rearrange("p (t c) -> p t c", c=P), ALU.add).then_inc(s_t0s, 1)
                    dve.wait_ge(s_t0s, b * J + j + 1)
                    for i in range(CT * j, CT * j + CT):
                        last = dve.bn_stats(stats[:, i, :], xt[:, i, :])
                    step(last, vb)
                    dve.sem_inc(s_none, 1)
                    for i in range(CT * j, CT * j + CT):
                        last = dve.bn_aggr(mv[:, i, :], stats[:, i, :])
                    step(last, vb)

                max_tiles(0)
                for j in range(J):
                    if j + 1 < J:
                        max_tiles(j + 1)
                    finish0(j)

                def norm(k):
                    dve.tensor_scalar(rstd[:, :], mv[:, :, 1], 1e-5, None, ALU.add).then_inc(s_var, 1)
                    dve.wait_ge(s_sqrt, b * 2 + k + 1)
                    step(dve.reciprocal(rstd[:, :], rstd[:, :]), vb)
                    step(dve.scalar_tensor_tensor(nmr[:, :], mv[:, :, 0], -1.0, rstd[:, :], ALU.mult, ALU.mult), vb)
                    for j in range(J):
                        if j >= 2:
                            dve.wait_ge(s_xhT, b * (2 * J) + k * J + j - 1)
                        for i in range(CT):
                            t = CT * j + i
                            last = dve.tensor_scalar(work[:, j % 2, P * i:P * i + P], xt[:, t, :], rstd[:, t:t + 1],
                                                     nmr[:, t:t + 1], ALU.mult, ALU.add)
                        last.then_inc(s_xh, 1)

                norm(0)
                for j in range(J):
                    dve.wait_ge(s_qkv1, b * J + j + 1)
                    dve.tensor_reduce(absk[:, j:j + 1], ps[:, 3, :], AX_X, ALU.max,
                                      apply_absolute_value=True).then_inc(s_absk, 1)
                    dve.tensor_reduce(absq[:, j:j + 1], ps[:, 2, :], AX_X, ALU.max, apply_absolute_value=True)
                    dve.tensor_tensor(v1[:, CT * j:CT * j + CT, :],
                                      ps[:, 4 + j % 2, :].rearrange("p (t c) -> p t c", c=P),
                                      bqkv_row[:, :].rearrange("p (c s) -> p s c", s=3)[:, 2:3, :]
                                      .broadcast_to([P, CT, P]), ALU.add).then_inc(s_v1, 1)
                    dve.wait_ge(s_khi, b * J + j + 1)
                    dve.scalar_tensor_tensor(lo[:, j % 2, :], ps[:, 3, :], bqkv[:, 1:2],
                                             hi[:, j % 2, :].bitcast(F32), ALU.add, ALU.subtract).then_inc(s_klo, 1)
                dve.wait_ge(s_klo, b * J + J)
                step(dve.tensor_reduce(bound[:, 0:1], absq[:, :], AX_X, ALU.max), vb)
                step(dve.tensor_reduce(bound[:, 1:2], absk[:, :], AX_X, ALU.max), vb)
                step(dve.tensor_tensor(bound[:, 0:2], bound[:, 0:2], bqkv_abs[:, 0:2], ALU.add), vb)
                dve.tensor_tensor(bound[:, 2:3], bound[:, 0:1], bound[:, 1:2], ALU.mult).then_inc(s_bnd, 1)
                dve.wait_ge(s_bm, b + 1)
                step(dve.tensor_reduce(flag[0:1, 0:1], ps[0:1, 6, 0:H], AX_X, ALU.max), vb)
                dve.tensor_scalar(flag[0:1, 1:2], flag[0:1, 0:1], SAFE * float(P) ** 0.5, None,
                                  ALU.is_lt).then_inc(s_flag, 1)

                def q_low(u, base, count):
                    dve.wait_ge(s_qhi, count)
                    dve.scalar_tensor_tensor(lo[:, u, :], ps[:, 4 + 2 * u, :], bqkv[:, 0:1],
                                             hi[:, u, :].bitcast(F32), ALU.add, ALU.subtract).then_inc(s_qlo, 1)

                q_low(0, vb, b * (J + 1) + 1)
                dve.wait_ge(s_bp, b * 2 + 2)
                dve.wait_ge(s_flag, b + 1)
                dve.sem_inc(s_none, 1)
                small = dve.value_load(flag[0:1, 1:2].bitcast(I32), min_val=0, max_val=1 << 30)
                with dve.Fori(0, LOOPS) as i:
                    g = b * LOOPS + i
                    gl = g * L_STEPS
                    lsteps = [0]

                    def lstep(ins):
                        lsteps[0] += 1
                        ins.then_inc(s_vl, 1)
                        dve.wait_ge(s_vl, gl + lsteps[0])

                    def evacuate(u):
                        dve.wait_ge(s_dg, g * (2 * T // GROUP) + (T // GROUP * (u + 1) + 1))
                        dve.wait_ge(s_pv1, g * (2 * T) + (T * u + T + RING))
                        rden, o = work[:, 0, :], work[:, 1, :]
                        lstep(dve.reciprocal(rden, ps[:, 5 + 2 * u, :]))
                        dve.tensor_tensor(o, ps[:, 4 + 2 * u, :], rden, ALU.mult).then_inc(s_o1, 1)
                        dve.wait_ge(s_pr, g * 2 + u + 1)
                        t = xt[:, bass.ds(i * (2 * CT) + CT * u, CT), :]
                        dve.tensor_tensor(t, t, ps[:, 5 + 2 * u, :].rearrange("p (t c) -> p t c", c=P),
                                          ALU.add).then_inc(s_t1, 1)

                    for u in range(2):
                        with dve.If(small > 0):
                            dve.memset(qst[96:97, u, :, :].bitcast(F32), 0.0).then_inc(s_shift, 1)
                            dve.sem_inc(s_gu, 2 * H * CT)
                            dve.sem_inc(s_gm, 1)
                        with dve.Else():
                            for h in range(H):
                                for qt in range(CT):
                                    for c in range(2):
                                        m = 2 * (CT * h + qt) + c
                                        dve.wait_ge(s_gs, g * (4 * H * CT) + 2 * H * CT * u + m + 1)
                                        dve.tensor_reduce(mx[:, qt, c:c + 1], ps[:, 0:4, :],
                                                          mybir.AxisListType.XY, ALU.max).then_inc(s_gu, 1)
                                dve.wait_ge(s_gu, g * (4 * H * CT) + 2 * H * CT * u + 2 * CT * (h + 1))
                                last = dve.tensor_reduce(mneg[:, h, :], mx[:, :, 0:2], AX_X, ALU.max, negate=True)
                            last.then_inc(s_gm, 1)
                            for h in range(H):
                                dve.wait_ge(s_gr, g * (2 * H) + H * u + h + 1)
                                last = dve.tensor_copy(qst[96:97, u, h, :], ps[96:97, h, :])
                            last.then_inc(s_shift, 1)
                        for G in range(T // GROUP):
                            n = T * u + GROUP * G
                            if u == 1 and G == 1:
                                evacuate(0)
                            dve.wait_ge(s_e1, g * (4 * T) + (2 * (n + 2) + 2))
                            dve.wait_ge(s_dg, g * (2 * T // GROUP) + (T // GROUP * u + G + 1))
                            dve.tensor_tensor(psum4[:, :, :], prob[:, 0, :, :], prob[:, 1, :, :], ALU.add).then_inc(s_sum, 1)
                            for r in range(2, GROUP):
                                dve.wait_ge(s_e1, g * (4 * T) + (2 * (n + r + 1) + 2))
                                dve.wait_ge(s_sum, g * (2 * T // GROUP * 3) + 3 * (T // GROUP * u + G) + 3 + r - 1)
                                dve.tensor_tensor(psum4[:, :, :], psum4[:, :, :], prob[:, r, :, :],
                                                  ALU.add).then_inc(s_sum, 1)
                            if G == 4:
                                q_low(1 - u, None, b * (J + 1) + i * 2 + (u + 2))
                    evacuate(1)
                    assert lsteps[0] == L_STEPS, lsteps

                dve.wait_ge(s_t1, b * J + J)
                for i in range(T):
                    last = dve.bn_stats(stats[:, i, :], xt[:, i, :])
                step(last, vb)
                dve.sem_inc(s_none, 1)
                for i in range(T):
                    last = dve.bn_aggr(mv[:, i, :], stats[:, i, :])
                step(last, vb)
                norm(1)
                dve.wait_ge(s_rl, b + 1)
                wide = [P, T, E]
                logit = work[:, 0, 0:T * E].rearrange("p (t e) -> p t e", e=E)
                pr = work[:, 1, 0:T * E].rearrange("p (t e) -> p t e", e=E)
                cand = work[:, 2, 0:T * E].rearrange("p (t e) -> p t e", e=E)
                sel = work[:, 3, 0:T * E].rearrange("p (t e) -> p t e", e=E)
                col = stats[:, :, 0:4]
                gate = psum4[:, 1:3, :].rearrange("p a b -> p (a b)").rearrange("p (t w) -> p t w", w=32)
                desc = con[:, C_DESC:C_DESC + E].unsqueeze(1).broadcast_to(wide)

                def over(c):
                    return col[:, :, c:c + 1].broadcast_to(wide)

                step(dve.tensor_tensor(logit, ps[:, 2, 0:T * E].rearrange("p (t e) -> p t e", e=E),
                                       rb[:, :].unsqueeze(1).broadcast_to(wide), ALU.add), vb)
                step(dve.tensor_reduce(col[:, :, 0], logit, AX_X, ALU.max), vb)
                dve.tensor_tensor(logit, logit, over(0), ALU.subtract).then_inc(s_rexpi, 1)
                dve.memset(psum4[:, 1:3, :], 0.0)
                dve.wait_ge(s_rexp, b + 1)
                step(dve.tensor_reduce(col[:, :, 0], logit, AX_X, ALU.add), vb)
                step(dve.reciprocal(col[:, :, 0], col[:, :, 0]), vb)
                step(dve.tensor_tensor(pr, logit, over(0), ALU.mult), vb)
                for r in range(2):
                    step(dve.tensor_reduce(col[:, :, 1 + r], pr, AX_X, ALU.max), vb)
                    step(dve.tensor_tensor(cand, pr, over(1 + r), ALU.is_equal), vb)
                    step(dve.tensor_tensor(cand, cand, desc, ALU.mult), vb)
                    step(dve.tensor_reduce(col[:, :, 3], cand, AX_X, ALU.max), vb)
                    step(dve.tensor_tensor(cand, cand, over(3), ALU.is_equal), vb)
                    if r == 0:
                        step(dve.tensor_tensor(sel, cand, pr, ALU.mult), vb)
                        step(dve.scalar_tensor_tensor(pr, cand, -2.0, pr, ALU.mult, ALU.add), vb)
                    else:
                        step(dve.tensor_tensor(cand, cand, pr, ALU.mult), vb)
                        step(dve.tensor_tensor(sel, sel, cand, ALU.add), vb)
                step(dve.tensor_tensor(col[:, :, 0], col[:, :, 1], col[:, :, 2], ALU.add), vb)
                step(dve.reciprocal(col[:, :, 0], col[:, :, 0]), vb)
                dve.tensor_tensor(gate[:, :, 0:E], sel, over(0), ALU.mult).then_inc(s_g, 1)
                dve.wait_ge(s_g, b + 1)
                vf = [0]

                def fstep(ins, lag):
                    vf[0] += 1
                    ins.then_inc(s_vf, 1)
                    dve.wait_ge(s_vf, b * F_STEPS + vf[0] - lag)

                odd = psum4[:, 3, 0:P]
                for j in range(J):
                    res = work[:, 2 + j % 2, :]
                    dve.wait_ge(s_eb, b * J + j + 1)
                    if j >= 2:
                        dve.wait_ge(s_out[j % 2], b * (8 * J) + 16 * (j // 2))
                    fstep(dve.tensor_tensor(res, xt[:, CT * j:CT * j + CT, :].rearrange("p t c -> p (t c)"),
                                            ps[:, 6 + j % 2, :], ALU.add), 0)
                    for i in range(CT):
                        t = CT * j + i
                        r = res[:, P * i:P * i + P]
                        dve.wait_ge(s_y, b * T + t + 1)
                        for e in range(E):
                            y = ps[:, 2 * (t % 3) + e // 4, P * (e % 4):P * (e % 4) + P]
                            ge = gate[:, t, e:e + 1]
                            if e == 1:
                                ins = dve.tensor_scalar(odd, y, ge, None, ALU.mult)
                            elif e % 2:
                                ins = dve.scalar_tensor_tensor(odd, y, ge, odd, ALU.mult, ALU.add)
                            else:
                                ins = dve.scalar_tensor_tensor(r, y, ge, r, ALU.mult, ALU.add)
                            fstep(ins, 0 if e == E - 1 else 1)
                        dve.sem_inc(s_yu, 1)
                        fstep(dve.tensor_tensor(r, r, odd, ALU.add), 0)
                    dve.sem_inc(s_r, 1)
                assert vf[0] == F_STEPS
                assert steps[0] == STEPS, steps
                dve.sem_inc(s_batch, 1)

        @block.tensor
        def _(pe):
            mm = nc.tensor.matmul
            pe.wait_ge(s_prep, PREP)
            pe.sem_inc(s_pv1, RING)
            pe.sem_inc(s_dg, 1)
            pe.sem_inc(s_batch, 1)
            with pe.Fori(0, B) as b:
                pe.wait_ge(s_batch, b * ENGINES + ENGINES)
                pe.sem_inc(s_none, 1)
                for j in range(J):
                    if j % 2 == 0:
                        pe.wait_ge(s_x[j // 2], b * 16 + 16)
                    if j >= 2:
                        pe.wait_ge(s_elu, b * J + j - 1)
                    for i in range(CT):
                        last = nc.tensor.transpose(ps[:, j % 2, P * i:P * i + P], xt[:, CT * j + i, :], ident)
                    last.then_inc(s_xT, 1)
                for j in range(J):
                    pe.wait_ge(s_elu, b * J + min(j + 2, J))
                    if j == 0:
                        pe.wait_ge(s_border, b * 7 + 2)
                        pe.wait_ge(s_cw[0], b * 16 + 16)
                    if j >= 2:
                        pe.wait_ge(s_c1, b * J + j - 1)
                    for k in range(9):
                        last = mm(ps[:, 2 + j % 2, :], w1[:, k, :], inner(c0, j, k // 3, k % 3),
                                  start=(k == 0), stop=(k == 8))
                    last.then_inc(s_conv1, 1)
                for j in range(J):
                    pe.wait_ge(s_c1, b * J + min(j + 2, J))
                    if j == 0:
                        pe.wait_ge(s_cw[1], b * 16 + 16)
                    if j >= 2:
                        pe.wait_ge(s_c3, b * J + j - 1)
                    for half in range(2):
                        for k in range(9):
                            last = mm(ps[:, 4 + 2 * half + j % 2, :], w2[:, k, P * half:P * half + P],
                                      inner(c1, j, k // 3, k % 3), start=(k == 0), stop=(k == 8))
                    last.then_inc(s_conv2, 1)
                pe.wait_ge(s_c3, b * J + J)
                for j in range(J):
                    if j:
                        pe.wait_ge(s_qk0s, b * J + j)
                    mm(ps[0:16, 0, :], wq0[:, :], c3[:, j, :], start=True, stop=True)
                    mm(ps[0:16, 1, :], wk0[:, :], c3[:, j, :], start=True, stop=True).then_inc(s_qk0, 1)
                    if j >= 2:
                        pe.wait_ge(s_v0, b * J + j - 1)
                    for i in range(CT):
                        last = mm(ps[:, 4 + j % 2, DV * i:DV * i + DV], c3[:, j, P * i:P * i + P], wv0[:, :],
                                  start=True, stop=True)
                    last.then_inc(s_v0m, 1)
                pe.wait_ge(s_qk0s, b * J + J)
                pe.wait_ge(s_v0, b * J + J)

                tile_no = [0]

                def max_tile(j, m):
                    qt, c = m // (j + 1), m % (j + 1)
                    k = tile_no[0]
                    tile_no[0] += 1
                    if k >= 2:
                        pe.wait_ge(s_mu, b * TILES0 + k - 1)
                    w = CH if c < j else (qt + 1) * P
                    mm(ps[:, k % 2, 0:w], q0[0:16, j, P * qt:P * qt + P], k0[0:16, c, 0:w],
                       start=True, stop=True).then_inc(s_ms, 1)

                def shift_row(j):
                    pe.wait_ge(s_mneg, b * J + j + 1)
                    for i in range(CT):
                        last = mm(ps[32:33, 7, P * i:P * i + P], mneg[:, 0, i:i + 1], ident, start=True, stop=True)
                    last.then_inc(s_mrow, 1)

                def scores0(j, i):
                    n = pair_of(j, i)
                    if n >= 2:
                        pe.wait_ge(s_e0, b * PAIRS0 + n - 1)
                    for k in range(2):
                        kt = 2 * i + k
                        last = mm(ps[:, 2 + 2 * (n % 2) + k, :], k0[0:33, kt // CT, P * (kt % CT):P * (kt % CT) + P],
                                  q0[0:33, j, :], start=True, stop=True)
                    last.then_inc(s_s0, 1)

                def values0(j, d):
                    n = pair_of(j, 2 * d)
                    pe.wait_ge(s_e0, b * PAIRS0 + n + 2)
                    if d == j:
                        pe.wait_ge(s_mask0, b * (CT * J) + CT * j + CT)
                    if d == 0 and j:
                        pe.wait_ge(s_acc0, b * J + j)
                    for g in range(4):
                        last = mm(ps[32 * g:32 * g + 32, 6, :], v0[:, 4 * d + g, :],
                                  prob[:, (n + g // 2) % RING, g % 2, :], start=(d == 0), stop=(d == j))
                    last.then_inc(s_pv0, 1)

                def finish0(j):
                    pe.wait_ge(s_acc0, b * J + j + 1)
                    pe.wait_ge(s_mu, b * TILES0 + tile_no[0])
                    mm(ps[:, 0, :], w3[:, :], work[:, 0, :], start=True, stop=True)
                    mm(ps[:, 1, :], con[:, C_DEN:C_DEN + P], work[:, 0, :], start=True, stop=True).then_inc(s_fin0, 1)
                    pe.wait_ge(s_t0, b * J + j + 1)
                    if j + 1 < J:
                        pe.wait_ge(s_mput, b * J + j + 2)
                    for i in range(CT):
                        last = nc.tensor.transpose(ps[:, 7, P * i:P * i + P], work[:, 3, P * i:P * i + P], ident)
                    last.then_inc(s_t0T, 1)

                for m in range(CT):
                    max_tile(0, m)
                shift_row(0)
                pe.wait_ge(s_mput, b * J + 1)
                for j in range(J):
                    pairs = 2 * (j + 1)
                    nxt = CT * (j + 2) if j + 1 < J else 0
                    done = 0
                    scores0(j, 0)
                    scores0(j, 1)
                    for d in range(j + 1):
                        while done < nxt * (d + 1) // (j + 1):
                            max_tile(j + 1, done)
                            done += 1
                        if d < j:
                            scores0(j, 2 * d + 2)
                            scores0(j, 2 * d + 3)
                        values0(j, d)
                    if j + 1 < J:
                        shift_row(j + 1)
                        pe.wait_ge(s_mput, b * J + j + 2)
                    finish0(j)
                    pe.wait_ge(s_t0s, b * J + j + 1)

                def norm(k):
                    for j in range(J):
                        n = k * J + j
                        pe.wait_ge(s_xh, b * (2 * J) + n + 1)
                        if j >= 2:
                            pe.wait_ge(s_xhs, b * (2 * J) + n - 1)
                        for i in range(CT):
                            last = nc.tensor.transpose(ps[:, j % 2, P * i:P * i + P], work[:, j % 2, P * i:P * i + P], ident)
                        last.then_inc(s_xhT, 1)

                norm(0)
                for j in range(J):
                    pe.wait_ge(s_xhs, b * (2 * J) + min(j + 1, J))
                    if j:
                        pe.wait_ge(s_klo, b * J + j)
                    xh = xhT[:, CH * j:CH * j + CH]
                    mm(ps[:, 2, :], ws(0), xh, start=True, stop=True)
                    mm(ps[:, 3, :], ws(1), xh, start=True, stop=True)
                    for i in range(CT):
                        last = mm(ps[:, 4 + j % 2, P * i:P * i + P], xh[:, P * i:P * i + P], ws(2), start=True, stop=True)
                    last.then_inc(s_qkv1, 1)
                pe.wait_ge(s_v1, b * J + J)
                pe.wait_ge(s_bnd, b + 1)
                pe.sem_inc(s_none, 1)
                mm(ps[0:1, 6, 0:H], bound[:, 2:3], con[:, C_HEAD:C_HEAD + H], start=True, stop=True).then_inc(s_bm, 1)
                mm(ps[:, 4, :], ws(0), xhT[:, 0:CH], start=True, stop=True).then_inc(s_qp, 1)
                pe.wait_ge(s_bp, b * 2 + 1)
                for q in range(2):
                    pe.wait_ge(s_kst[q], b * (12 * 16 * J // 2) + 12 * 16 * J // 2)
                pe.wait_ge(s_flag, b + 1)
                pe.sem_inc(s_none, 1)
                small = pe.value_load(flag[0:1, 1:2].bitcast(I32), min_val=0, max_val=1 << 30)
                with pe.Fori(0, LOOPS) as i:
                    g = b * LOOPS + i

                    def scores1(u, kt):
                        for h in range(H):
                            if h % 2 == 0:
                                pe.wait_ge(s_e1, g * (4 * T) + (2 * (T * u + kt) + h // 2 + 1))
                            last = mm(ps[:, h, :], kst[0:97, h, P * kt:P * kt + P], qst[0:97, u, h, :],
                                      start=True, stop=True)
                            if h % 2:
                                last.then_inc(s_s1, 1)

                    def values1(u, kt):
                        pe.wait_ge(s_e1, g * (4 * T) + (2 * (T * u + kt) + 4))
                        for h in range(H):
                            last = mm(ps[D * h:D * h + D, 4 + 2 * u, :], v1[:, kt, D * h:D * h + D],
                                      prob[:, kt % RING, h, :], start=(kt == 0), stop=(kt == T - 1))
                        last.then_inc(s_pv1, 1)

                    def sums1(u, G):
                        pe.wait_ge(s_sum, g * (2 * T // GROUP * 3) + 3 * (T // GROUP * u + G + 1) + 3)
                        for h in range(H):
                            last = mm(ps[D * h:D * h + D, 5 + 2 * u, :], ones32[:, :], psum4[:, h, :],
                                      start=(G == 0), stop=(G == T // GROUP - 1))
                        last.then_inc(s_dg, 1)

                    def project1(u):
                        pe.wait_ge(s_o1, g * 2 + u + 1)
                        for k in range(CT):
                            last = mm(ps[:, 5 + 2 * u, P * k:P * k + P], work[:, 1, P * k:P * k + P], wproj[:, :],
                                      start=True, stop=True)
                        last.then_inc(s_pr, 1)

                    for u in range(2):
                        if u == 0:
                            pe.wait_ge(s_qst[0], b * (192 * (LOOPS + 1)) + i * 192 + 192)
                        else:
                            pe.wait_ge(s_qst[1], g * 192 + 192)
                        pe.sem_inc(s_none, 1)
                        with pe.If(small > 0):
                            pe.sem_inc(s_gs, 2 * H * CT)
                            pe.sem_inc(s_gr, H)
                        with pe.Else():
                            for h in range(H):
                                for qt in range(CT):
                                    for c in range(2):
                                        m = 2 * (CT * h + qt) + c
                                        if m == 0:
                                            pe.wait_ge(s_e1, g * (4 * T) + (2 * T * u + 2))
                                        else:
                                            pe.wait_ge(s_gu, g * (4 * H * CT) + 2 * H * CT * u + m)
                                        for k in range(4):
                                            last = mm(ps[:, k, :], qst[0:96, u, h, P * qt:P * qt + P],
                                                      kst[0:96, h, CH * (4 * c + k):CH * (4 * c + k) + CH],
                                                      start=True, stop=True)
                                        last.then_inc(s_gs, 1)
                            pe.wait_ge(s_gm, g * 2 + u + 1)
                            for h in range(H):
                                for qt in range(CT):
                                    last = mm(ps[96:97, h, P * qt:P * qt + P], mneg[:, h, qt:qt + 1], ident,
                                              start=True, stop=True)
                                last.then_inc(s_gr, 1)
                        pe.wait_ge(s_shift, g * 2 + u + 1)
                        for kt in range(T):
                            scores1(u, kt)
                            if kt:
                                values1(u, kt - 1)
                            if kt >= 6 and (kt - 6) % GROUP == 0:
                                sums1(u, (kt - 6) // GROUP)
                            if u == 1 and kt == 7:
                                project1(0)
                            if kt == 10:
                                if u == 1:
                                    pe.wait_ge(s_t1, b * J + i * 2 + 1)
                                nxt = xhT[:, bass.ds(i * (2 * CH) + CH * (u + 1), CH)]
                                mm(ps[:, 4 + 2 * (1 - u), :], ws(0), nxt, start=True, stop=True).then_inc(s_qp, 1)
                        values1(u, T - 1)
                        sums1(u, T // GROUP - 1)
                    project1(1)
                norm(1)
                for j in range(J):
                    pe.wait_ge(s_xhs, b * (2 * J) + J + j + 1)
                    for k in range(CT):
                        t = CT * j + k
                        last = mm(ps[:, 2, E * t:E * t + E], xhT[:, P * t:P * t + P], rw[:, :], start=True, stop=True)
                last.then_inc(s_rl, 1)
                pe.wait_ge(s_g, b + 1)
                gate = psum4[:, 1:3, :].rearrange("p a b -> p (a b)")
                for k in range(J):
                    last = nc.tensor.transpose(ps[:, 3 + k // 4, P * (k % 4):P * (k % 4) + P],
                                               gate[:, P * k:P * k + P], ident)
                last.then_inc(s_gT, 1)
                pe.wait_ge(s_gTs, b + 1)
                for j in range(J):
                    if j >= 2:
                        pe.wait_ge(s_r, b * J + j - 1)
                    gT = (work[:, 1, :] if j < 4 else psum4[:, 0, :])[:, P * (j % 4):P * (j % 4) + P]
                    for k in range(CT):
                        last = mm(ps[:, 6 + j % 2, P * k:P * k + P], gT, eb[:, k, :],
                                  start=True, stop=True)
                    last.then_inc(s_eb, 1)
                    for k in range(CT):
                        t = CT * j + k
                        if t >= 3:
                            pe.wait_ge(s_yu, b * T + t - 2)
                        for half in range(2):
                            last = mm(ps[:, 2 * (t % 3) + half, :], xhT[:, P * t:P * t + P],
                                      ew[:, 4 * half:4 * half + 4, :], start=True, stop=True)
                        last.then_inc(s_y, 1)
                pe.wait_ge(s_y, b * T + T)
                pe.sem_inc(s_batch, 1)


_INS = ["x", "L0_conv_W1", "L0_conv_b1", "L0_conv_W2", "L0_conv_b2", "L0_conv_Wq", "L0_conv_bq", "L0_conv_Wk",
        "L0_conv_bk", "L0_conv_Wv", "L0_conv_bv", "L0_conv_W3", "L0_conv_b3", "L1_attn_W_qkv", "L1_attn_b_qkv",
        "L1_attn_W_proj", "L1_attn_b_proj", "L1_ffn_router_w", "L1_ffn_router_b", "L1_ffn_expert_w",
        "L1_ffn_expert_b"]


def kernel(**inputs):
    import numpy as np
    import concourse.bacc as bacc
    from concourse.bass_utils import run_bass_kernel_spmd

    nc = bacc.Bacc("TRN2", target_bir_lowering=False, num_devices=1)
    arrays, args = {}, {}
    for name in _INS:
        arrays[f"in_{name}"] = np.ascontiguousarray(inputs[name])
        args[name] = nc.dram_tensor(f"in_{name}", arrays[f"in_{name}"].shape, F32, kind="ExternalInput").ap()
    arrays["in_constants"] = constants()
    consts = nc.dram_tensor("in_constants", (P, C_COLS), F32, kind="ExternalInput").ap()
    out = nc.dram_tensor("out_0", (B, IMG, IMG, P), F32, kind="ExternalOutput").ap()
    conv_hybrid_kernel(nc, args, consts, out)
    r = run_bass_kernel_spmd(nc, [arrays], core_ids=[0])
    return r.results[0]["out_0"]
```

```python
from contextlib import ExitStack

import concourse.bass as bass
from concourse import mybir

ALU = mybir.AluOpType
ACT = mybir.ActivationFunctionType
F32 = mybir.dt.float32
F32R = mybir.dt.float32r
I32 = mybir.dt.int32
AX_X = mybir.AxisListType.X

P = 128
IMG = 64
PAD = IMG + 2
N = IMG * IMG
B = 4
T = N // P
CH = 512
J = N // CH
CT = CH // P
ROWS = CH // IMG
H, D = 4, 32
DQK, DV = 4, 16
E = 8
RING = 4
GROUP_AT = [0, 6, 11, 16, 21, 26, T]
SAFE = 60.0

C_ID, C_TRI, C_TRI0, C_DEN, C_MASK, C_HEAD, C_DESC, C_COLS = 0, 128, 640, 768, 769, 771, 775, 783


def constants():
    import numpy as np
    c = np.zeros((P, C_COLS), np.float32)
    p = np.arange(P)
    c[:, C_ID:C_ID + P] = np.eye(P)
    tri = np.where(p[None, :] < p[:, None], 0.0, -4.0e10)
    c[:, C_TRI + CH - P:C_TRI + CH] = tri
    c[:, C_TRI0:C_TRI0 + P] = tri
    c[0, C_TRI0] = 0.0
    c[DV::32, C_DEN] = 1.0
    c[0:16, C_MASK] = [(r // DQK) % 2 for r in range(16)]
    c[0:16, C_MASK + 1] = [r // (2 * DQK) for r in range(16)]
    c[p, C_HEAD + p // D] = 1.0
    c[:, C_DESC:C_DESC + E] = np.arange(E, 0, -1)
    return c


PAIRS0 = sum(2 * (j + 1) for j in range(J))
TILES0 = sum(CT * (j + 1) for j in range(J))
QUADS0 = PAIRS0 // 2
STEPS = 71
LOOPS = J // 2 - 1
HALF = N // 2
GROUPS1 = len(GROUP_AT) - 1
SUMS1 = T - GROUPS1
FIRST, LAST = 0, J - 1
INVERT_AT, DIVIDE_AT, PROJECT_AT, RESIDUAL_AT = [4, 7, 9, 12], 14, 17, 19
Q_AT_TILE, Q_LOW_AT = 22, 23
SUM_LAG = 2
Q_AT = J // 2 - 1
F_STEPS = J * (3 + CT * (E // 2))
ENGINES = 5


def group_of(kt):
    return max(g for g in range(GROUPS1) if GROUP_AT[g] <= kt)


def sums_with(kt):
    g = group_of(kt)
    return GROUP_AT[g] - g + max(kt - GROUP_AT[g], 1)


SUM_CREDIT = SUMS1 + 1 - sums_with(T - RING)


def conv_hybrid_kernel(nc, a, consts, out):
    with ExitStack() as ctx:
        def sb(name, shape, dt=F32):
            return ctx.enter_context(nc.sbuf_tensor(name, shape, dt))

        def sem(name):
            return ctx.enter_context(nc.semaphore(name))

        ps = ctx.enter_context(nc.psum_tensor("ps", [P, 8, CH], F32))

        con = sb("con", [P, C_COLS])
        b1 = sb("b1", [P, 1])
        b2 = sb("b2", [P, 2])
        b2h = sb("b2h", [P, 1])
        wq0 = sb("wq0", [P, 16])
        wk0 = sb("wk0", [P, 16])
        wv0 = sb("wv0", [P, DV])
        bqk0 = sb("bqk0", [16, 2])
        bqk0m = sb("bqk0m", [16, 2])
        bv0 = sb("bv0", [P, DV])
        w3 = sb("w3", [P, P + 1])
        b3 = sb("b3", [P, P])
        rden0 = sb("rden0", [P, CT])
        wqkv = sb("wqkv", [P, 3 * P])
        bqkv = sb("bqkv", [P, 3])
        bqkv_abs = sb("bqkv_abs", [P, 3])
        bqkv_row = sb("bqkv_row", [P, 3 * P])
        wproj = sb("wproj", [P, P])
        bproj = sb("bproj", [P, P])
        rw = sb("rw", [P, E])
        rb = sb("rb", [P, E])
        ew = sb("ew", [P, E, P])
        eb = sb("eb", [P, CT, P])
        ones32 = sb("ones32", [P, 32])

        xt = sb("xt", [P, T, P])
        prob = sb("prob", [P, RING, H, CH])
        psum4 = sb("psum4", [P, H, CH])
        w3all = psum4[:, 0:2, :].rearrange("p a b -> p (a b)").rearrange("p (h c) -> p h c", c=P)
        work = sb("work", [P, 4, CH])
        mv = sb("mv", [P, T, 2])
        stats = sb("stats", [P, T, 6])
        rstd = sb("rstd", [P, T])
        nmr = sb("nmr", [P, T])
        mx = sb("mx", [P, CT, J])
        mneg = sb("mneg", [P, H, CT])
        absq = sb("absq", [P, J])
        absk = sb("absk", [P, J])
        bound = sb("bound", [P, 4])
        flag = sb("flag", [1, 8])
        xhT = sb("xhT", [P, N])
        ring = prob[:, :, :, :].rearrange("p r h c -> p (r h c)")
        xin = ring[:, 0:N].rearrange("p (t c) -> p t c", c=P)
        gates = psum4[:, 1:3, :].rearrange("p a b -> p (a b)").rearrange("p (t w) -> p t w", w=32)
        scaled = ring[:, N:2 * N].rearrange("p (u e n) -> p u e n", u=2, e=E // 2)
        kparts = ring.rearrange("p (f s n) -> p f s n", f=2, s=2)
        early = ExitStack()

        def sbe(name, shape, dt=F32):
            return early.enter_context(nc.sbuf_tensor(name, shape, dt))

        w1 = sbe("w1", [P, 9, P])
        w2 = sbe("w2", [P, 9, 2 * P])
        c0 = sbe("c0", [P, PAD, PAD])
        c1 = sbe("c1", [P, PAD, PAD])
        c3 = sbe("c3", [P, J, CH])
        q0 = sbe("q0", [33, J, CH], F32R)
        k0 = sbe("k0", [33, J, CH], F32R)
        v0 = sbe("v0", [P, T, 32])
        early.close()
        kst = sb("kst", [P, H, N], F32R)
        qst = sb("qst", [P, 2, H, CH], F32R)
        hi = sb("hi", [P, 2, CH], F32R)
        lo = sb("lo", [P, 2, CH], F32R)
        v1 = sb("v1", [P, T, P])

        mh0 = ps[:, 0:2, 0:2 * (P + 1)].rearrange("p b (t c) -> p b t c", c=P + 1)
        ident = con[:, C_ID:C_ID + P]

        s_w = sem("weights_loaded")
        s_zero = sem("rows_zeroed")
        s_prep = sem("weights_ready")
        s_batch = sem("batch_done")
        s_none = sem("unused")
        s_x = [sem(f"x_loaded{q}") for q in range(4)]
        s_cw = [sem(f"conv_weights_loaded{q}") for q in range(2)]
        s_xcp = sem("x_copied")
        s_border = sem("borders_zero")
        s_xT = sem("x_transposed")
        s_min = sem("min_done")
        s_eexp = sem("elu_exp_done")
        s_elu = sem("elu_done")
        s_conv1 = sem("conv1_summed")
        s_c1 = sem("conv1_stored")
        s_conv2 = sem("conv2_summed")
        s_tanh = sem("tanh_done")
        s_c3 = sem("gated_done")
        s_qk0 = sem("qk0_multiplied")
        s_hm0 = sem("qk0_high_parts")
        s_qk0s = sem("qk0_stacked")
        s_v0m = sem("v0_multiplied")
        s_v0 = sem("v0_stored")
        s_ms = sem("max_scores")
        s_mu = sem("max_taken")
        s_mneg = sem("shift0_done")
        s_mrow = sem("shift0_row")
        s_mput = sem("shift0_stored")
        s_s0 = sem("scores0")
        s_e0 = sem("exp0_done")
        s_mask0 = sem("exp0_masked")
        s_pv0 = sem("pv0_done")
        s_acc0 = sem("acc0_copied")
        s_fin0 = sem("mh0_multiplied")
        s_t0 = sem("t0_transposed_ready")
        s_t0T = sem("t0_transposed")
        s_t0s = sem("t0_stored")
        s_var = sem("variance_ready")
        s_sqrt = sem("sqrt_done")
        s_xh = sem("normalised")
        s_xhT = sem("normalised_transposed")
        s_xhs = sem("normalised_stored")
        s_qkv1 = sem("qkv1_multiplied")
        s_absk = sem("k1_bound_taken")
        s_khi = sem("k1_high_done")
        s_klo = sem("k1_low_done")
        s_v1 = sem("v1_stored")
        s_kst = [sem(f"k_stacked{q}") for q in range(2)]
        s_bm = sem("bound_multiplied")
        s_bnd = sem("bound_ready")
        s_flag = sem("flag_ready")
        s_bp = sem("proj_bias_added")
        s_qp = sem("q1_multiplied")
        s_qhi = sem("q1_high_done")
        s_qlo = sem("q1_low_done")
        s_qst = [sem(f"q_stacked{q}") for q in range(2)]
        s_gs = sem("general_scores")
        s_gu = sem("general_max_taken")
        s_gm = sem("general_shift_done")
        s_gr = sem("general_shift_row")
        s_shift = sem("shift_stored")
        s_s1 = sem("scores1")
        s_e1 = sem("exp1_done")
        s_pv1 = sem("pv1_done")
        s_sum = sem("group_sums")
        s_dg = sem("group_sums_used")
        s_o1 = sem("attention_out")
        s_dc = sem("den1_inverted")
        s_pr = sem("projected")
        s_t1 = sem("t1_stored")
        s_rl = sem("router_multiplied")
        s_rexpi = sem("router_exp_ready")
        s_rexp = sem("router_exp_done")
        s_g = sem("gates_ready")
        s_gT = sem("gates_transposed")
        s_gTs = sem("gates_stored")
        s_eb = sem("expert_bias_multiplied")
        s_y = sem("expert_multiplied")
        s_yu = sem("first_experts_used")
        s_ys = sem("last_experts_scaled")
        s_ya = sem("last_experts_added")
        s_ebu = sem("expert_bias_used")
        s_r = sem("result_ready")
        s_out = [sem(f"stored{q}") for q in range(2)]
        s_v = sem("vector_steps")
        s_vf = sem("vector_combine_steps")

        x_tok = a["x"].rearrange("b h w c -> b (h w) c").rearrange("b (t p) c -> b p t c", p=P)
        out_tok = out.rearrange("b h w c -> b (h w) c").rearrange("b (t p) c -> b p t c", p=P)

        weight_loads = [
            (con[:, :], consts),
            (b1[:, :], a["L0_conv_b1"].rearrange("(c o) -> c o", o=1)),
            (b2[:, 0:1], a["L0_conv_b2"][0:P].rearrange("(c o) -> c o", o=1)),
            (b2[:, 1:2], a["L0_conv_b2"][P:2 * P].rearrange("(c o) -> c o", o=1)),
            (wv0[:, :], a["L0_conv_Wv"]),
            (bv0[:, :], a["L0_conv_bv"].partition_broadcast(P)),
            (b3[:, :], a["L0_conv_b3"].partition_broadcast(P)),
            (wqkv[:, :], a["L1_attn_W_qkv"]),
            (bqkv[:, :], a["L1_attn_b_qkv"].rearrange("(c s) -> c s", s=3)),
            (bqkv_row[:, :], a["L1_attn_b_qkv"].partition_broadcast(P)),
            (wproj[:, :], a["L1_attn_W_proj"]),
            (bproj[:, :], a["L1_attn_b_proj"].partition_broadcast(P)),
            (rw[:, :], a["L1_ffn_router_w"]),
            (rb[:, :], a["L1_ffn_router_b"].partition_broadcast(P)),
            (ew[:, :, :], a["L1_ffn_expert_w"].rearrange("e d c -> d e c")),
        ]
        for g in range(4):
            weight_loads += [
                (wq0[:, DQK * g:DQK * g + DQK], a["L0_conv_Wq"]),
                (wk0[:, DQK * g:DQK * g + DQK], a["L0_conv_Wk"]),
                (bqk0[DQK * g:DQK * g + DQK, 0:1], a["L0_conv_bq"].rearrange("(c o) -> c o", o=1)),
                (bqk0[DQK * g:DQK * g + DQK, 1:2], a["L0_conv_bk"].rearrange("(c o) -> c o", o=1)),
                (w3all[32 * g:32 * g + DV, :, :], a["L0_conv_W3"].rearrange("(h d) c -> d h c", d=DV)),
                (eb[32 * g:32 * g + E, g, :], a["L1_ffn_expert_b"]),
            ]
        PREP = 3

        def ws(s):
            return wqkv[:, :].rearrange("p (c s) -> p s c", s=3)[:, s, :]

        def inner(padded, j, dy=1, dx=1):
            return padded[:, ROWS * j + dy:ROWS * j + dy + ROWS, dx:dx + IMG]

        def rows(ap):
            return ap.rearrange("p (r w) -> p r w", w=IMG)

        def kpart(j, part):
            at = CH * (j % (J // 2))
            return kparts[:, 2 * j // J, part, at:at + CH]

        def pair_of(j, i):
            return j * (j + 1) + i

        block = ctx.enter_context(nc.Block())

        @block.sync
        def _(sp):
            sp.wait_ge(s_zero, 2)
            for dst, src in weight_loads:
                sp.dma_start(dst, src).then_inc(s_w, 16)

            def load_batch(b):
                for q in range(4):
                    sp.dma_start(xin[:, 8 * q:8 * q + 8, :], x_tok[b][:, 8 * q:8 * q + 8, :]).then_inc(s_x[q], 16)
                sp.dma_start(w1[:, :, :], a["L0_conv_W1"].rearrange("kh kw i o -> i (kh kw) o")).then_inc(s_cw[0], 16)
                sp.dma_start(w2[:, :, :], a["L0_conv_W2"].rearrange("kh kw i o -> i (kh kw) o")).then_inc(s_cw[1], 16)

            def stack_queries(b, c, u):
                sp.wait_ge(s_qlo, b * J + (c + 1))
                for h in range(H):
                    for g, part in enumerate((hi, lo, hi)):
                        sp.dma_start(qst[32 * g:32 * g + D, u, h, :].bitcast(F32),
                                     part[D * h:D * h + D, u, :].bitcast(F32)).then_inc(s_qst[u], 16)

            def batch(b, last):
                sp.wait_ge(s_batch, b * ENGINES + ENGINES)
                sp.sem_inc(s_none, 1)
                for f in range(2):
                    sp.wait_ge(s_klo, b * J + (J // 2) * (f + 1))
                    for h in range(H):
                        for g, part in enumerate((0, 0, 1)):
                            sp.dma_start(kst[32 * g:32 * g + D, h, HALF * f:HALF * f + HALF].bitcast(F32),
                                         kparts[D * h:D * h + D, f, part, :]).then_inc(s_kst[f], 16)
                    if f == 0:
                        stack_queries(b, 0, 0)
                with sp.Fori(0, LOOPS) as i:
                    stack_queries(b, i * 2 + 1, 1)
                    stack_queries(b, i * 2 + 2, 0)
                stack_queries(b, J - 1, 1)
                if not last:
                    sp.wait_ge(s_t1, b * J + J)
                    sp.sem_inc(s_none, 1)
                    load_batch(b + 1)
                for j in range(J):
                    sp.wait_ge(s_r, b * J + j + 1)
                    sp.dma_start(out_tok[b][:, CT * j:CT * j + CT, :],
                                 work[:, 2 + j % 2, :].rearrange("p (t c) -> p t c", c=P)).then_inc(s_out[j % 2], 16)
                for q in range(2):
                    sp.wait_ge(s_out[q], b * (8 * J) + 8 * J)
                sp.sem_inc(s_batch, 1)

            load_batch(0)
            sp.sem_inc(s_batch, 1)
            with sp.Fori(0, B - 1) as b:
                batch(b, False)
            batch(B - 1, True)

        @block.gpsimd
        def _(pool):
            pool.memset(w3all[:, :, :], 0.0).then_inc(s_zero, 1)
            pool.memset(eb[:, :, :], 0.0).then_inc(s_zero, 1)

            def prepare(b):
                for c in (c0, c1):
                    pool.memset(c[:, 0, :], 0.0)
                    pool.memset(c[:, PAD - 1, :], 0.0)
                    pool.memset(c[:, 1:PAD - 1, 0:1], 0.0)
                    pool.memset(c[:, 1:PAD - 1, PAD - 1:PAD], 0.0).then_inc(s_border, 1)
                pool.memset(q0[:, :, :].bitcast(F32), 0.0).then_inc(s_border, 1)
                pool.memset(k0[:, :, :].bitcast(F32), 0.0).then_inc(s_border, 1)
                pool.memset(v0[:, :, DV + 1:32], 0.0)
                pool.memset(v0[:, :, DV:DV + 1], 1.0).then_inc(s_border, 1)
                pool.wait_ge(s_border, b * 7 + 5)
                pool.sem_inc(s_none, 1)
                pool.memset(k0[32:33, :, :].bitcast(F32), 1.0).then_inc(s_border, 1)
                pool.wait_ge(s_border, b * 7 + 6)
                pool.sem_inc(s_border, 1)

            prepare(0)
            pool.sem_inc(s_batch, 1)
            with pool.Fori(0, B) as b:
                pool.wait_ge(s_batch, b * ENGINES + ENGINES)
                pool.sem_inc(s_none, 1)
                for q in range(4):
                    pool.wait_ge(s_x[q], b * 16 + 16)
                pool.sem_inc(s_none, 1)
                pool.tensor_tensor(xt[:, :, :], xin, b3[:, :].unsqueeze(1).broadcast_to([P, T, P]),
                                   ALU.add).then_inc(s_xcp, 1)
                for j in range(J):
                    for i in range(CT):
                        n = pair_of(j, 2 * j + i // 2)
                        pool.wait_ge(s_e0, b * PAIRS0 + n + 1)
                        pool.sem_inc(s_none, 1)
                        tile = prob[:, n % RING, i % 2, 0:(i + 1) * P]
                        pool.affine_select(out=tile, in_=tile, pattern=[[1, (i + 1) * P]],
                                           compare_op=ALU.is_gt, fill=0.0, base=-P * i,
                                           channel_multiplier=-1).then_inc(s_mask0, 1)
                pool.wait_ge(s_t0s, b * J + 1)
                pool.wait_ge(s_mask0, b * (CT * J) + CT * J)
                pool.sem_inc(s_none, 1)
                pool.memset(kst[96:97, 0:3, :].bitcast(F32), 1.0)
                pool.wait_ge(s_t0s, b * J + J)
                pool.sem_inc(s_none, 1)
                pool.memset(qst[96:97, :, :, :].bitcast(F32), 0.0)
                pool.memset(kst[96:97, 3, :].bitcast(F32), 1.0).then_inc(s_bp, 1)
                pool.wait_ge(s_bp, b * 2 + 1)
                pool.wait_ge(s_xh, b * (2 * J) + J)
                pool.sem_inc(s_none, 1)
                pool.tensor_tensor(xt[:, :, :], xt[:, :, :],
                                   bproj[:, :].unsqueeze(1).broadcast_to([P, T, P]), ALU.add).then_inc(s_bp, 1)
                pool.wait_ge(s_t1, b * J + J)
                pool.sem_inc(s_none, 1)
                prepare(b + 1)
                for j in range(J):
                    u = j % 2
                    pool.wait_ge(s_ys, b * T + CT * (j + 1))
                    pool.sem_inc(s_none, 1)
                    pool.tensor_tensor(scaled[:, u, 0:2, :], scaled[:, u, 0:2, :], scaled[:, u, 2:4, :],
                                       ALU.add).then_inc(s_ya, 1)
                    pool.wait_ge(s_ya, b * (2 * J) + 2 * j + 1)
                    pool.sem_inc(s_none, 1)
                    pool.tensor_tensor(scaled[:, u, 0, :], scaled[:, u, 0, :], scaled[:, u, 1, :],
                                       ALU.add).then_inc(s_ya, 1)
                pool.wait_ge(s_ya, b * (2 * J) + 2 * J)
                pool.sem_inc(s_none, 1)
                pool.sem_inc(s_batch, 1)

        @block.scalar
        def _(act):
            act.wait_ge(s_prep, PREP)
            act.sem_inc(s_e1, 2)
            act.sem_inc(s_batch, 1)
            with act.Fori(0, B) as b:
                act.wait_ge(s_batch, b * ENGINES + ENGINES)
                act.sem_inc(s_none, 1)
                def elu_exp(j):
                    act.wait_ge(s_min, b * J + j + 1)
                    act.activation(work[:, 2 + j % 2, :], work[:, j % 2, :], ACT.Exp).then_inc(s_eexp, 1)

                for j in range(3):
                    elu_exp(j)
                for j in range(J):
                    act.wait_ge(s_conv1, b * J + j + 1)
                    if j == 0:
                        act.wait_ge(s_border, b * 7 + 2)
                    act.activation(inner(c1, j), rows(ps[:, 2 + j % 2, :]), ACT.Identity,
                                   bias=b1[:, 0:1]).then_inc(s_c1, 1)
                    if j + 3 < J:
                        elu_exp(j + 3)
                def high0(j):
                    act.wait_ge(s_qk0, b * J + j + 1)
                    if j:
                        act.wait_ge(s_qk0s, b * J + j)
                    for s in range(2):
                        last = act.activation(work[0:16, 2 + s, :].bitcast(F32R), ps[0:16, s, :], ACT.Identity,
                                              bias=bqk0m[:, s:s + 1], scale=con[0:16, C_MASK + s:C_MASK + s + 1])
                    last.then_inc(s_hm0, 1)

                for j in range(J):
                    act.wait_ge(s_conv2, b * J + j + 1)
                    if j >= 2:
                        act.wait_ge(s_c3, b * J + j - 1)
                    act.activation(work[:, j % 2, :], ps[:, 6 + j % 2, :], ACT.Tanh, scale=0.5,
                                   bias=b2h[:, 0:1]).then_inc(s_tanh, 1)
                    if j:
                        high0(j - 1)
                high0(J - 1)
                act.wait_ge(s_xcp, b + 1)

                def keep_acc0(j):
                    act.wait_ge(s_pv0, b * QUADS0 + pair_of(j, 2 * (j + 1)) // 2)
                    if j:
                        act.wait_ge(s_fin0, b * J + j)
                    act.activation(work[:, 0, :], ps[:, 6, :], ACT.Copy).then_inc(s_acc0, 1)

                for j in range(J):
                    for i in range(2 * (j + 1)):
                        n = pair_of(j, i)
                        act.wait_ge(s_s0, b * PAIRS0 + n + 1)
                        if n >= RING:
                            act.wait_ge(s_pv0, b * QUADS0 + (n - RING) // 2 + 1)
                        bank = 2 + 2 * (n % 2)
                        act.activation(prob[:, n % RING, 0:2, :], ps[:, bank:bank + 2, :], ACT.Exp,
                                       scale=0.25).then_inc(s_e0, 1)
                        if i == 1 and j:
                            keep_acc0(j - 1)
                keep_acc0(J - 1)

                def deviations(k):
                    act.wait_ge(s_var, b * 2 + k + 1)
                    act.activation(rstd[:, :], rstd[:, :], ACT.Sqrt).then_inc(s_sqrt, 1)

                def keep_normalised(k, j):
                    act.wait_ge(s_xhT, b * (2 * J) + k * J + j + 1)
                    act.activation(xhT[:, CH * j:CH * j + CH], ps[:, j % 2, :], ACT.Copy).then_inc(s_xhs, 1)

                def k_high(j):
                    act.wait_ge(s_absk, b * J + j + 1)
                    act.activation(kpart(j, 0).bitcast(F32R), ps[:, 3 + 4 * (j % 2), :], ACT.Identity,
                                   bias=bqkv[:, 1:2]).then_inc(s_khi, 1)

                def q_high(c, u):
                    act.wait_ge(s_qp, b * J + (c + 1))
                    act.sem_inc(s_none, 1)
                    act.activation(hi[:, u, :], ps[:, 4 + 2 * u, :], ACT.Identity, bias=bqkv[:, 0:1]).then_inc(s_qhi, 1)

                deviations(0)
                for j in range(J):
                    keep_normalised(0, j)
                    if j:
                        k_high(j - 1)
                        if j - 1 == Q_AT:
                            q_high(FIRST, 0)
                k_high(J - 1)

                def chunk(c, u):
                    C = b * J + c
                    for kt in range(T):
                        act.wait_ge(s_pv1, C * T + (kt + 1))
                        reader = sums_with(kt - RING) if kt >= RING else sums_with(kt - RING + T) - SUMS1
                        act.wait_ge(s_sum, C * SUMS1 + (reader + SUM_CREDIT))
                        if c is FIRST and kt in (0, 2):
                            act.wait_ge(s_kst[kt // 2], b * 192 + 192)
                        for h2 in range(2):
                            act.wait_ge(s_s1, C * (2 * T) + (2 * kt + h2 + 1))
                            act.activation(prob[:, kt % RING, 2 * h2:2 * h2 + 2, :], ps[:, 2 * h2:2 * h2 + 2, :],
                                           ACT.Exp, scale=float(P) ** -0.5).then_inc(s_e1, 1)
                        if kt == Q_AT_TILE and c is not LAST:
                            q_high(c + 1, 1 - u)

                chunk(FIRST, 0)
                with act.Fori(0, LOOPS) as i:
                    chunk(i * 2 + 1, 1)
                    chunk(i * 2 + 2, 0)
                chunk(LAST, 1)
                act.wait_ge(s_t1, b * J + J)
                deviations(1)
                for j in range(J):
                    keep_normalised(1, j)
                act.wait_ge(s_rexpi, b + 1)
                act.sem_inc(s_none, 1)
                act.activation(work[:, 0, 0:T * E], work[:, 0, 0:T * E], ACT.Exp).then_inc(s_rexp, 1)
                act.wait_ge(s_gT, b + 1)
                act.activation(work[:, 1, :], ps[:, 3, :], ACT.Copy)
                act.activation(psum4[:, 0, :], ps[:, 4, :], ACT.Copy).then_inc(s_gTs, 1)
                act.wait_ge(s_gTs, b + 1)
                for t in range(T):
                    j, at = t // CT, P * (t % CT)
                    act.wait_ge(s_y, b * T + t + 1)
                    if j >= 2 and t % CT == 0:
                        act.wait_ge(s_r, b * J + j - 1)
                    for e in range(E // 2):
                        last = act.activation(scaled[:, j % 2, e, at:at + P], ps[:, 2 * (t % 3) + 1, P * e:P * e + P],
                                              ACT.Identity, scale=gates[:, t, E // 2 + e:E // 2 + e + 1])
                    last.then_inc(s_ys, 1)
                act.wait_ge(s_ys, b * T + T)
                act.sem_inc(s_batch, 1)

        @block.vector
        def _(dve):
            steps = [0]

            def step(ins, base):
                steps[0] += 1
                ins.then_inc(s_v, 1)
                dve.wait_ge(s_v, base + steps[0])

            dve.memset(ones32[:, :], 1.0).then_inc(s_prep, 1)
            dve.wait_ge(s_w, 16 * len(weight_loads))
            dve.tensor_copy(w3[:, P:P + 1], con[:, C_DEN:C_DEN + 1])
            dve.tensor_reduce(w3[:, 0:P], w3all[:, :, :].rearrange("p h c -> p c h"), AX_X, ALU.add)
            dve.tensor_scalar(b2h[:, :], b2[:, 1:2], 0.5, None, ALU.mult)
            dve.scalar_tensor_tensor(bqkv_abs[:, :], bqkv[:, :], -1.0, bqkv[:, :], ALU.mult, ALU.max).then_inc(s_prep, 1)
            dve.tensor_tensor(bqk0m[:, :], bqk0[:, :], con[0:16, C_MASK:C_MASK + 2], ALU.mult).then_inc(s_prep, 1)
            dve.wait_ge(s_prep, PREP)
            dve.sem_inc(s_sum, SUM_CREDIT)
            dve.sem_inc(s_batch, 1)
            with dve.Fori(0, B) as b:
                vb = b * STEPS
                dve.wait_ge(s_batch, b * ENGINES + ENGINES)
                dve.sem_inc(s_none, 1)

                def elu_min(j):
                    dve.wait_ge(s_xT, b * J + j + 1)
                    dve.tensor_scalar(work[:, j % 2, :], ps[:, j % 2, :], 0.0, None, ALU.min).then_inc(s_min, 1)

                dve.wait_ge(s_border, b * 7 + 1)
                elu_min(0)
                for j in range(J):
                    if j + 1 < J:
                        elu_min(j + 1)
                    dve.wait_ge(s_eexp, b * J + j + 1)
                    dve.scalar_tensor_tensor(inner(c0, j), rows(work[:, 2 + j % 2, :]), -1.0,
                                             rows(ps[:, j % 2, :]), ALU.add, ALU.max).then_inc(s_elu, 1)
                def gated(j):
                    dve.wait_ge(s_tanh, b * J + j + 1)
                    gate = work[:, j % 2, :]
                    step(dve.tensor_scalar(gate, gate, 0.5, 0.5, ALU.mult, ALU.add), vb)
                    dve.scalar_tensor_tensor(c3[:, j, :], ps[:, 4 + j % 2, :], b2[:, 0:1], gate,
                                             ALU.add, ALU.mult).then_inc(s_c3, 1)

                def split0(j):
                    dve.wait_ge(s_hm0, b * J + j + 1)
                    for s, dst in enumerate((q0, k0)):
                        last = dve.scalar_tensor_tensor(dst[0:16, j, :], ps[0:16, s, :], bqk0[:, s:s + 1],
                                                        work[0:16, 2 + s, :], ALU.add, ALU.subtract)
                    last.then_inc(s_qk0s, 1)
                    dve.wait_ge(s_v0m, b * J + j + 1)
                    dve.tensor_tensor(v0[:, CT * j:CT * j + CT, 0:DV],
                                      ps[:, 2 + j % 2, 0:CT * DV].rearrange("p (t d) -> p t d", d=DV),
                                      bv0[:, :].unsqueeze(1).broadcast_to([P, CT, DV]), ALU.add).then_inc(s_v0, 1)

                dve.wait_ge(s_border, b * 7 + 7)
                for j in range(J):
                    gated(j)
                    if j:
                        split0(j - 1)
                split0(J - 1)

                tile_no = [0]

                def max_tiles(j):
                    for qt in range(CT):
                        for c in range(j + 1):
                            m = tile_no[0]
                            tile_no[0] += 1
                            dve.wait_ge(s_ms, b * TILES0 + m + 1)
                            if c < j:
                                ins = dve.tensor_reduce(mx[:, qt, c:c + 1], ps[:, m % 2, :], AX_X, ALU.max)
                            else:
                                dve.sem_inc(s_none, 1)
                                w = (qt + 1) * P
                                mask = con[:, C_TRI0:C_TRI0 + P] if j == qt == 0 else con[:, C_TRI + CH - w:C_TRI + CH]
                                ins = dve.tensor_tensor_reduce(out=ps[:, m % 2, 0:w], in0=ps[:, m % 2, 0:w], in1=mask,
                                                               scale=1.0, scalar=-3.0e38, op0=ALU.add, op1=ALU.max,
                                                               accum_out=mx[:, qt, c:c + 1])
                            ins.then_inc(s_mu, 1)
                    dve.wait_ge(s_mu, b * TILES0 + tile_no[0])
                    if j >= 2:
                        dve.wait_ge(s_mrow, b * J + j - 1)
                    dve.tensor_reduce(mneg[:, j % 2, :], mx[:, :, 0:j + 1], AX_X, ALU.max, negate=True)\
                       .then_inc(s_mneg, 1)
                    dve.wait_ge(s_mneg, b * J + j + 1)

                def keep_shift(j):
                    dve.wait_ge(s_mrow, b * J + j + 1)
                    dve.tensor_copy(q0[32:33, j, :], ps[32:33, 7, :]).then_inc(s_mput, 1)

                def divide0(j):
                    dve.wait_ge(s_fin0, b * J + j + 1)
                    step(dve.tensor_scalar(rden0[:, :], mh0[:, :, :, P], 1e-10, None, ALU.add), vb)
                    step(dve.reciprocal(rden0[:, :], rden0[:, :]), vb)
                    for i in range(CT):
                        t = xt[:, CT * j + i, :]
                        last = dve.scalar_tensor_tensor(t, mh0[:, i // 2, i % 2, 0:P], rden0[:, i:i + 1], t,
                                                        ALU.mult, ALU.add)
                    last.then_inc(s_t0, 1)

                def residual0(j):
                    dve.wait_ge(s_t0T, b * J + j + 1)
                    dve.wait_ge(s_t0, b * J + j + 1)
                    t = xt[:, CT * j:CT * j + CT, :]
                    dve.tensor_tensor(t, t, ps[:, 7, :].rearrange("p (t c) -> p t c", c=P), ALU.add).then_inc(s_t0s, 1)
                    dve.wait_ge(s_t0s, b * J + j + 1)
                    for i in range(CT * j, CT * j + CT):
                        last = dve.bn_stats(stats[:, i, :], xt[:, i, :])
                    step(last, vb)
                    dve.sem_inc(s_none, 1)
                    for i in range(CT * j, CT * j + CT):
                        last = dve.bn_aggr(mv[:, i, :], stats[:, i, :])
                    step(last, vb)

                max_tiles(0)
                max_tiles(1)
                keep_shift(0)
                keep_shift(1)
                dve.wait_ge(s_xcp, b + 1)
                for j in range(J):
                    if j:
                        divide0(j - 1)
                        if j + 1 < J:
                            keep_shift(j + 1)
                    if j + 2 < J:
                        max_tiles(j + 2)
                    if j:
                        residual0(j - 1)
                divide0(J - 1)
                residual0(J - 1)

                def norm(k):
                    dve.tensor_scalar(rstd[:, :], mv[:, :, 1], 1e-5, None, ALU.add).then_inc(s_var, 1)
                    dve.wait_ge(s_sqrt, b * 2 + k + 1)
                    step(dve.reciprocal(rstd[:, :], rstd[:, :]), vb)
                    step(dve.scalar_tensor_tensor(nmr[:, :], mv[:, :, 0], -1.0, rstd[:, :], ALU.mult, ALU.mult), vb)

                def normalise(k, j):
                    if j >= 2:
                        dve.wait_ge(s_xhT, b * (2 * J) + k * J + j - 1)
                    for i in range(CT):
                        t = CT * j + i
                        last = dve.tensor_scalar(work[:, j % 2, P * i:P * i + P], xt[:, t, :], rstd[:, t:t + 1],
                                                 nmr[:, t:t + 1], ALU.mult, ALU.add)
                    last.then_inc(s_xh, 1)

                def keys(j):
                    dve.wait_ge(s_qkv1, b * J + j + 1)
                    dve.tensor_reduce(absk[:, j:j + 1], ps[:, 3 + 4 * (j % 2), :], AX_X, ALU.max,
                                      apply_absolute_value=True).then_inc(s_absk, 1)
                    dve.tensor_reduce(absq[:, j:j + 1], ps[:, 2 + 4 * (j % 2), :], AX_X, ALU.max, apply_absolute_value=True)
                    dve.tensor_tensor(v1[:, CT * j:CT * j + CT, :],
                                      ps[:, 4 + j % 2, :].rearrange("p (t c) -> p t c", c=P),
                                      bqkv_row[:, :].rearrange("p (c s) -> p s c", s=3)[:, 2:3, :]
                                      .broadcast_to([P, CT, P]), ALU.add).then_inc(s_v1, 1)
                    dve.wait_ge(s_khi, b * J + j + 1)
                    dve.scalar_tensor_tensor(kpart(j, 1).bitcast(F32R), ps[:, 3 + 4 * (j % 2), :], bqkv[:, 1:2], kpart(j, 0),
                                             ALU.add, ALU.subtract).then_inc(s_klo, 1)

                def q_low(c, u):
                    dve.wait_ge(s_qhi, b * J + (c + 1))
                    dve.scalar_tensor_tensor(lo[:, u, :], ps[:, 4 + 2 * u, :], bqkv[:, 0:1],
                                             hi[:, u, :].bitcast(F32), ALU.add, ALU.subtract).then_inc(s_qlo, 1)

                norm(0)
                for j in range(2):
                    normalise(0, j)
                for j in range(J):
                    if j + 2 < J:
                        normalise(0, j + 2)
                    keys(j)
                    if j == Q_AT:
                        q_low(FIRST, 0)
                dve.wait_ge(s_klo, b * J + J)
                step(dve.tensor_reduce(bound[:, 0:1], absq[:, :], AX_X, ALU.max), vb)
                step(dve.tensor_reduce(bound[:, 1:2], absk[:, :], AX_X, ALU.max), vb)
                step(dve.tensor_tensor(bound[:, 0:2], bound[:, 0:2], bqkv_abs[:, 0:2], ALU.add), vb)
                dve.tensor_tensor(bound[:, 2:3], bound[:, 0:1], bound[:, 1:2], ALU.mult).then_inc(s_bnd, 1)
                dve.wait_ge(s_bm, b + 1)
                step(dve.tensor_reduce(flag[0:1, 0:1], ps[0:1, 6, 0:H], AX_X, ALU.max), vb)
                dve.tensor_scalar(flag[0:1, 1:2], flag[0:1, 0:1], SAFE * float(P) ** 0.5, None,
                                  ALU.is_lt).then_inc(s_flag, 1)

                dve.wait_ge(s_bp, b * 2 + 2)
                dve.wait_ge(s_flag, b + 1)
                dve.sem_inc(s_none, 1)
                small = dve.value_load(flag[0:1, 1:2].bitcast(I32), min_val=0, max_val=1 << 30)

                def invert1(c, u, k):
                    dve.wait_ge(s_dg, (b * J + c) * GROUPS1 + (GROUPS1 + 1))
                    dve.reciprocal(work[:, 0, P * k:P * k + P], ps[:, 5 + 2 * u, P * k:P * k + P]).then_inc(s_dc, 1)

                def divide1(c, u):
                    dve.wait_ge(s_pv1, (b * J + c) * T + (T + RING))
                    dve.wait_ge(s_dc, (b * J + c) * 4 + 4)
                    dve.tensor_tensor(work[:, 1, :], ps[:, 4 + 2 * u, :], work[:, 0, :], ALU.mult).then_inc(s_o1, 1)

                def residual1(c, u):
                    dve.wait_ge(s_pr, b * J + (c + 1))
                    t = xt[:, bass.ds(c * CT, CT), :]
                    dve.tensor_tensor(t, t, ps[:, 5 + 2 * u, :].rearrange("p (t c) -> p t c", c=P),
                                      ALU.add).then_inc(s_t1, 1)
                    dve.wait_ge(s_t1, b * J + (c + 1))
                    dve.sem_inc(s_none, 1)
                    st = stats[:, bass.ds(c * CT, CT), :]
                    for i in range(CT):
                        last = dve.bn_stats(st[:, i, :], t[:, i, :])
                    return last

                def chunk(c, u):
                    C = b * J + c
                    with dve.If(small > 0):
                        dve.sem_inc(s_shift, 1)
                        dve.sem_inc(s_gu, 2 * H * CT)
                        dve.sem_inc(s_gm, 1)
                    with dve.Else():
                        for h in range(H):
                            for qt in range(CT):
                                for half in range(2):
                                    m = 2 * (CT * h + qt) + half
                                    dve.wait_ge(s_gs, C * (2 * H * CT) + (m + 1))
                                    dve.tensor_reduce(mx[:, qt, 2 * h + half:2 * h + half + 1], ps[:, 0:4, :],
                                                      mybir.AxisListType.XY, ALU.max).then_inc(s_gu, 1)
                        dve.wait_ge(s_gu, C * (2 * H * CT) + 2 * H * CT)
                        for h in range(H):
                            last = dve.tensor_reduce(mneg[:, h, :], mx[:, :, 2 * h:2 * h + 2], AX_X, ALU.max,
                                                     negate=True)
                        last.then_inc(s_gm, 1)
                        for h in range(H):
                            dve.wait_ge(s_gr, C * H + (h + 1))
                            last = dve.tensor_copy(qst[96:97, u, h, :], ps[96:97, h, :])
                        last.then_inc(s_shift, 1)
                    for kt in range(1, T):
                        G = group_of(kt)
                        r = kt - GROUP_AT[G]
                        if r == 0:
                            continue
                        dve.wait_ge(s_e1, C * (2 * T) + (2 * (kt + 1) + 2))
                        if r == 1:
                            dve.wait_ge(s_dg, C * GROUPS1 + (G + 1))
                            dve.tensor_tensor(psum4[:, :, :], prob[:, (kt - 1) % RING, :, :], prob[:, kt % RING, :, :],
                                              ALU.add).then_inc(s_sum, 1)
                        else:
                            dve.wait_ge(s_sum, C * SUMS1 + (sums_with(kt) - 1 + SUM_CREDIT))
                            dve.tensor_tensor(psum4[:, :, :], psum4[:, :, :], prob[:, kt % RING, :, :],
                                              ALU.add).then_inc(s_sum, 1)
                        if c is not FIRST:
                            if kt in INVERT_AT:
                                invert1(c - 1, 1 - u, INVERT_AT.index(kt))
                            elif kt == DIVIDE_AT:
                                divide1(c - 1, 1 - u)
                            elif kt == RESIDUAL_AT:
                                residual1(c - 1, 1 - u)
                        if kt == Q_LOW_AT and c is not LAST:
                            q_low(c + 1, 1 - u)

                chunk(FIRST, 0)
                with dve.Fori(0, LOOPS) as i:
                    chunk(i * 2 + 1, 1)
                    chunk(i * 2 + 2, 0)
                chunk(LAST, 1)
                for k in range(4):
                    invert1(LAST, 1, k)
                divide1(LAST, 1)
                step(residual1(LAST, 1), vb)
                dve.sem_inc(s_none, 1)
                for i in range(T):
                    last = dve.bn_aggr(mv[:, i, :], stats[:, i, :])
                step(last, vb)
                norm(1)
                for j in range(J):
                    normalise(1, j)
                dve.wait_ge(s_rl, b + 1)
                wide = [P, T, E]
                logit = work[:, 0, 0:T * E].rearrange("p (t e) -> p t e", e=E)
                pr = work[:, 1, 0:T * E].rearrange("p (t e) -> p t e", e=E)
                cand = work[:, 2, 0:T * E].rearrange("p (t e) -> p t e", e=E)
                sel = work[:, 3, 0:T * E].rearrange("p (t e) -> p t e", e=E)
                col = stats[:, :, 0:4]
                desc = con[:, C_DESC:C_DESC + E].unsqueeze(1).broadcast_to(wide)

                def over(c):
                    return col[:, :, c:c + 1].broadcast_to(wide)

                step(dve.tensor_tensor(logit, ps[:, 2, 0:T * E].rearrange("p (t e) -> p t e", e=E),
                                       rb[:, :].unsqueeze(1).broadcast_to(wide), ALU.add), vb)
                step(dve.tensor_reduce(col[:, :, 0], logit, AX_X, ALU.max), vb)
                dve.tensor_tensor(logit, logit, over(0), ALU.subtract).then_inc(s_rexpi, 1)
                dve.memset(psum4[:, 1:3, :], 0.0)
                dve.wait_ge(s_rexp, b + 1)
                step(dve.tensor_reduce(col[:, :, 0], logit, AX_X, ALU.add), vb)
                step(dve.reciprocal(col[:, :, 0], col[:, :, 0]), vb)
                step(dve.tensor_tensor(pr, logit, over(0), ALU.mult), vb)
                for r in range(2):
                    step(dve.tensor_reduce(col[:, :, 1 + r], pr, AX_X, ALU.max), vb)
                    step(dve.tensor_tensor(cand, pr, over(1 + r), ALU.is_equal), vb)
                    step(dve.tensor_tensor(cand, cand, desc, ALU.mult), vb)
                    step(dve.tensor_reduce(col[:, :, 3], cand, AX_X, ALU.max), vb)
                    step(dve.tensor_tensor(cand, cand, over(3), ALU.is_equal), vb)
                    if r == 0:
                        step(dve.tensor_tensor(sel, cand, pr, ALU.mult), vb)
                        step(dve.scalar_tensor_tensor(pr, cand, -2.0, pr, ALU.mult, ALU.add), vb)
                    else:
                        step(dve.tensor_tensor(cand, cand, pr, ALU.mult), vb)
                        step(dve.tensor_tensor(sel, sel, cand, ALU.add), vb)
                step(dve.tensor_tensor(col[:, :, 0], col[:, :, 1], col[:, :, 2], ALU.add), vb)
                step(dve.reciprocal(col[:, :, 0], col[:, :, 0]), vb)
                dve.tensor_tensor(gates[:, :, 0:E], sel, over(0), ALU.mult).then_inc(s_g, 1)
                dve.wait_ge(s_g, b + 1)
                vf = [0]

                def fstep(ins, lag):
                    vf[0] += 1
                    ins.then_inc(s_vf, 1)
                    dve.wait_ge(s_vf, b * F_STEPS + vf[0] - lag)

                def odd(j):
                    return psum4[:, 3, :] if j % 2 else work[:, 0, :]

                def finish(j):
                    res = work[:, 2 + j % 2, :]
                    fstep(dve.tensor_tensor(res, res, odd(j), ALU.add), 0)
                    dve.wait_ge(s_ya, b * (2 * J) + 2 * j + 2)
                    fstep(dve.tensor_tensor(res, res, scaled[:, j % 2, 0, :], ALU.add), 0)
                    dve.sem_inc(s_r, 1)

                for j in range(J):
                    res = work[:, 2 + j % 2, :]
                    dve.wait_ge(s_eb, b * J + j + 1)
                    if j >= 2:
                        dve.wait_ge(s_out[j % 2], b * (8 * J) + 16 * (j // 2))
                    fstep(dve.tensor_tensor(res, xt[:, CT * j:CT * j + CT, :].rearrange("p t c -> p (t c)"),
                                            ps[:, 6 + j % 2, :], ALU.add), 0)
                    dve.sem_inc(s_ebu, 1)
                    for i in range(CT):
                        t = CT * j + i
                        cols = slice(P * i, P * i + P)
                        dve.wait_ge(s_y, b * T + t + 1)
                        for e in range(E // 2):
                            y = ps[:, 2 * (t % 3), P * e:P * e + P]
                            ge = gates[:, t, e:e + 1]
                            if e == 1:
                                ins = dve.tensor_scalar(odd(j)[:, cols], y, ge, None, ALU.mult)
                            else:
                                r = odd(j)[:, cols] if e % 2 else res[:, cols]
                                ins = dve.scalar_tensor_tensor(r, y, ge, r, ALU.mult, ALU.add)
                            fstep(ins, 0 if e == E // 2 - 1 else 1)
                        dve.sem_inc(s_yu, 1)
                        if i == 1 and j:
                            finish(j - 1)
                finish(J - 1)
                assert vf[0] == F_STEPS
                assert steps[0] == STEPS, steps
                dve.sem_inc(s_batch, 1)

        @block.tensor
        def _(pe):
            mm = nc.tensor.matmul
            pe.wait_ge(s_prep, PREP)
            pe.sem_inc(s_pv1, RING)
            pe.sem_inc(s_dg, 1)
            pe.sem_inc(s_batch, 1)
            with pe.Fori(0, B) as b:
                pe.wait_ge(s_batch, b * ENGINES + ENGINES)
                pe.sem_inc(s_none, 1)
                def x_to_channels(j):
                    if j % 2 == 0:
                        pe.wait_ge(s_x[j // 2], b * 16 + 16)
                    if j >= 2:
                        pe.wait_ge(s_elu, b * J + j - 1)
                    for i in range(CT):
                        last = nc.tensor.transpose(ps[:, j % 2, P * i:P * i + P], xin[:, CT * j + i, :], ident)
                    last.then_inc(s_xT, 1)
                for j in range(3):
                    x_to_channels(j)
                for j in range(J):
                    pe.wait_ge(s_elu, b * J + min(j + 2, J))
                    if j == 0:
                        pe.wait_ge(s_border, b * 7 + 2)
                        pe.wait_ge(s_cw[0], b * 16 + 16)
                    if j >= 2:
                        pe.wait_ge(s_c1, b * J + j - 1)
                    for k in range(9):
                        last = mm(ps[:, 2 + j % 2, :], w1[:, k, :], inner(c0, j, k // 3, k % 3),
                                  start=(k == 0), stop=(k == 8))
                    last.then_inc(s_conv1, 1)
                    if j + 3 < J:
                        x_to_channels(j + 3)
                def project0(j):
                    pe.wait_ge(s_c3, b * J + j + 1)
                    if j:
                        pe.wait_ge(s_qk0s, b * J + j)
                    mm(ps[0:16, 0, :], wq0[:, :], c3[:, j, :], start=True, stop=True)
                    mm(ps[0:16, 1, :], wk0[:, :], c3[:, j, :], start=True, stop=True).then_inc(s_qk0, 1)
                    if j >= 2:
                        pe.wait_ge(s_v0, b * J + j - 1)
                    for i in range(CT):
                        last = mm(ps[:, 2 + j % 2, DV * i:DV * i + DV], c3[:, j, P * i:P * i + P], wv0[:, :],
                                  start=True, stop=True)
                    last.then_inc(s_v0m, 1)

                for j in range(J):
                    pe.wait_ge(s_c1, b * J + min(j + 2, J))
                    if j == 0:
                        pe.wait_ge(s_cw[1], b * 16 + 16)
                    if j >= 2:
                        pe.wait_ge(s_c3, b * J + j - 1)
                    for half in range(2):
                        for k in range(9):
                            last = mm(ps[:, 4 + 2 * half + j % 2, :], w2[:, k, P * half:P * half + P],
                                      inner(c1, j, k // 3, k % 3), start=(k == 0), stop=(k == 8))
                    last.then_inc(s_conv2, 1)
                    if j == 1:
                        pe.wait_ge(s_c1, b * J + J)
                    if j:
                        project0(j - 1)
                project0(J - 1)
                pe.wait_ge(s_qk0s, b * J + J)
                pe.wait_ge(s_v0, b * J + J)

                tile_no = [0]

                def max_tile(j, m):
                    qt, c = m // (j + 1), m % (j + 1)
                    k = tile_no[0]
                    tile_no[0] += 1
                    if k >= 2:
                        pe.wait_ge(s_mu, b * TILES0 + k - 1)
                    w = CH if c < j else (qt + 1) * P
                    mm(ps[:, k % 2, 0:w], q0[0:16, j, P * qt:P * qt + P], k0[0:16, c, 0:w],
                       start=True, stop=True).then_inc(s_ms, 1)

                def shift_row(j):
                    pe.wait_ge(s_mneg, b * J + j + 1)
                    if j == 1:
                        pe.wait_ge(s_mput, b * J + 1)
                    if j >= 3:
                        pe.wait_ge(s_t0s, b * J + j - 2)
                    for i in range(CT):
                        last = mm(ps[32:33, 7, P * i:P * i + P], mneg[:, j % 2, i:i + 1], ident, start=True, stop=True)
                    last.then_inc(s_mrow, 1)

                def scores0(j, i):
                    n = pair_of(j, i)
                    if n >= 2:
                        pe.wait_ge(s_e0, b * PAIRS0 + n - 1)
                    for k in range(2):
                        kt = 2 * i + k
                        last = mm(ps[:, 2 + 2 * (n % 2) + k, :], k0[0:33, kt // CT, P * (kt % CT):P * (kt % CT) + P],
                                  q0[0:33, j, :], start=True, stop=True)
                    last.then_inc(s_s0, 1)

                def values0(j, d):
                    n = pair_of(j, 2 * d)
                    pe.wait_ge(s_e0, b * PAIRS0 + n + 2)
                    if d == j:
                        pe.wait_ge(s_mask0, b * (CT * J) + CT * j + CT)
                    if d == 0 and j:
                        pe.wait_ge(s_acc0, b * J + j)
                    for g in range(4):
                        last = mm(ps[32 * g:32 * g + 32, 6, :], v0[:, 4 * d + g, :],
                                  prob[:, (n + g // 2) % RING, g % 2, :], start=(d == 0), stop=(d == j))
                    last.then_inc(s_pv0, 1)

                def finish0(j):
                    pe.wait_ge(s_acc0, b * J + j + 1)
                    pe.wait_ge(s_mu, b * TILES0 + tile_no[0])
                    if j:
                        pe.wait_ge(s_t0, b * J + j)
                    for i in range(CT):
                        last = mm(mh0[:, i // 2, i % 2, :], work[:, 0, P * i:P * i + P], w3[:, :],
                                  start=True, stop=True)
                    last.then_inc(s_fin0, 1)

                def to_tokens0(j):
                    pe.wait_ge(s_mput, b * J + min(j + 3, J))
                    if j:
                        pe.wait_ge(s_t0s, b * J + j)
                    for i in range(CT):
                        last = nc.tensor.transpose(ps[:, 7, P * i:P * i + P], c3[:, j, P * i:P * i + P], ident)
                    last.then_inc(s_t0T, 1)

                for j in range(2):
                    for m in range(CT * (j + 1)):
                        max_tile(j, m)
                for j in range(2):
                    shift_row(j)
                quads = [(j, d) for j in range(J) for d in range(j + 1)]
                pe.wait_ge(s_mput, b * J + 1)
                scores0(0, 0)
                scores0(0, 1)
                for q, (j, d) in enumerate(quads):
                    tiles = CT * (j + 3) if j + 2 < J else 0
                    first, end = tiles * d // (j + 1), tiles * (d + 1) // (j + 1)
                    cut = [first, first + (end - first) // 3, first + 2 * (end - first) // 3] if d else [first] * 3
                    if q + 1 < len(quads):
                        nj, nd = quads[q + 1]
                        if nd == 0:
                            pe.wait_ge(s_mput, b * J + nj + 1)
                        for i in range(1 if d == 0 and j else 2):
                            scores0(nj, 2 * nd + i)
                            for m in range(cut[i], cut[i + 1]):
                                max_tile(j + 2, m)
                    values0(j, d)
                    if d == 0 and j:
                        finish0(j - 1)
                        if j + 1 < J:
                            shift_row(j + 1)
                        scores0(nj, 2 * nd + 1)
                        if tiles:
                            pe.wait_ge(s_t0, b * J + j)
                    for m in range(cut[2], end):
                        max_tile(j + 2, m)
                    if d == j and j:
                        to_tokens0(j - 1)
                finish0(J - 1)
                to_tokens0(J - 1)
                pe.wait_ge(s_t0s, b * J + J)

                def to_channels(k, j):
                    n = k * J + j
                    pe.wait_ge(s_xh, b * (2 * J) + n + 1)
                    if j >= 2:
                        pe.wait_ge(s_xhs, b * (2 * J) + n - 1)
                    for i in range(CT):
                        last = nc.tensor.transpose(ps[:, j % 2, P * i:P * i + P], work[:, j % 2, P * i:P * i + P], ident)
                    last.then_inc(s_xhT, 1)

                to_channels(0, 0)
                for j in range(J):
                    if j + 1 < J:
                        to_channels(0, j + 1)
                    pe.wait_ge(s_xhs, b * (2 * J) + j + 1)
                    if j >= 2:
                        pe.wait_ge(s_klo, b * J + j - 1)
                    xh = xhT[:, CH * j:CH * j + CH]
                    if j == Q_AT + 1:
                        pe.wait_ge(s_qlo, b * J + 1)
                    mm(ps[:, 2 + 4 * (j % 2), :], ws(0), xh, start=True, stop=True)
                    mm(ps[:, 3 + 4 * (j % 2), :], ws(1), xh, start=True, stop=True)
                    for i in range(CT):
                        last = mm(ps[:, 4 + j % 2, P * i:P * i + P], xh[:, P * i:P * i + P], ws(2), start=True, stop=True)
                    last.then_inc(s_qkv1, 1)
                    if j == Q_AT:
                        pe.wait_ge(s_v1, b * J + Q_AT)
                        mm(ps[:, 4, :], ws(0), xhT[:, 0:CH], start=True, stop=True).then_inc(s_qp, 1)
                pe.wait_ge(s_v1, b * J + J)
                pe.wait_ge(s_bnd, b + 1)
                pe.sem_inc(s_none, 1)
                mm(ps[0:1, 6, 0:H], bound[:, 2:3], con[:, C_HEAD:C_HEAD + H], start=True, stop=True).then_inc(s_bm, 1)
                pe.wait_ge(s_bp, b * 2 + 1)
                pe.wait_ge(s_flag, b + 1)
                pe.sem_inc(s_none, 1)
                small = pe.value_load(flag[0:1, 1:2].bitcast(I32), min_val=0, max_val=1 << 30)

                def scores1(C, u, kt, pair):
                    pe.wait_ge(s_e1, C * (2 * T) + (2 * kt + pair + 1))
                    for h in (2 * pair, 2 * pair + 1):
                        last = mm(ps[:, h, :], kst[0:97, h, P * kt:P * kt + P], qst[0:97, u, h, :],
                                  start=True, stop=True)
                    last.then_inc(s_s1, 1)

                def values1(C, u, kt):
                    pe.wait_ge(s_e1, C * (2 * T) + (2 * kt + 4))
                    for h in range(H):
                        last = mm(ps[D * h:D * h + D, 4 + 2 * u, :], v1[:, kt, D * h:D * h + D],
                                  prob[:, kt % RING, h, :], start=(kt == 0), stop=(kt == T - 1))
                    last.then_inc(s_pv1, 1)

                def sums1(C, u, G):
                    pe.wait_ge(s_sum, C * SUMS1 + (GROUP_AT[G + 1] - (G + 1) + SUM_CREDIT))
                    for h in range(H):
                        last = mm(ps[D * h:D * h + D, 5 + 2 * u, :], ones32[:, :], psum4[:, h, :],
                                  start=(G == 0), stop=(G == GROUPS1 - 1))
                    last.then_inc(s_dg, 1)

                def project1(c, u):
                    pe.wait_ge(s_o1, b * J + (c + 1))
                    for k in range(CT):
                        last = mm(ps[:, 5 + 2 * u, P * k:P * k + P], work[:, 1, P * k:P * k + P], wproj[:, :],
                                  start=True, stop=True)
                    last.then_inc(s_pr, 1)

                def general_maxima(C, u):
                    for f in range(2):
                        pe.wait_ge(s_kst[f], b * 192 + 192)
                    for h in range(H):
                        for qt in range(CT):
                            for half in range(2):
                                m = 2 * (CT * h + qt) + half
                                if m == 0:
                                    pe.wait_ge(s_e1, C * (2 * T) + 2)
                                else:
                                    pe.wait_ge(s_gu, C * (2 * H * CT) + m)
                                for k in range(4):
                                    at = CH * (4 * half + k)
                                    last = mm(ps[:, k, :], qst[0:96, u, h, P * qt:P * qt + P],
                                              kst[0:96, h, at:at + CH], start=True, stop=True)
                                last.then_inc(s_gs, 1)
                    pe.wait_ge(s_gm, C + 1)
                    for h in range(H):
                        for qt in range(CT):
                            last = mm(ps[96:97, h, P * qt:P * qt + P], mneg[:, h, qt:qt + 1], ident,
                                      start=True, stop=True)
                        last.then_inc(s_gr, 1)

                def chunk(c, u):
                    C = b * J + c
                    at = b * (96 * J) + (c - u) * 96 + 192
                    pe.wait_ge(s_qst[u], at)
                    pe.sem_inc(s_none, 1)
                    with pe.If(small > 0):
                        pe.sem_inc(s_gs, 2 * H * CT)
                        pe.sem_inc(s_gr, H)
                    with pe.Else():
                        general_maxima(C, u)
                        pe.wait_ge(s_shift, C + 1)
                    for kt in range(T):
                        if c is FIRST and kt in (0, T // 2):
                            pe.wait_ge(s_kst[2 * kt // T], b * 192 + 192)
                        scores1(C, u, kt, 0)
                        if kt >= 2:
                            values1(C, u, kt - 2)
                        elif c is not FIRST:
                            values1(C - 1, 1 - u, T + kt - 2)
                        scores1(C, u, kt, 1)
                        if kt - SUM_LAG in GROUP_AT[1:]:
                            sums1(C, u, GROUP_AT.index(kt - SUM_LAG) - 1)
                        elif kt == SUM_LAG and c is not FIRST:
                            sums1(C - 1, 1 - u, GROUPS1 - 1)
                        if kt == PROJECT_AT and c is not FIRST:
                            project1(c - 1, 1 - u)
                        if kt == Q_AT_TILE and c is not LAST:
                            if c is not FIRST:
                                pe.wait_ge(s_t1, C)
                            mm(ps[:, 4 + 2 * (1 - u), :], ws(0), xhT[:, bass.ds((c + 1) * CH, CH)],
                               start=True, stop=True).then_inc(s_qp, 1)

                chunk(FIRST, 0)
                with pe.Fori(0, LOOPS) as i:
                    chunk(i * 2 + 1, 1)
                    chunk(i * 2 + 2, 0)
                chunk(LAST, 1)
                for kt in (T - 2, T - 1):
                    values1(b * J + LAST, 1, kt)
                sums1(b * J + LAST, 1, GROUPS1 - 1)
                project1(LAST, 1)
                to_channels(1, 0)
                for j in range(J):
                    if j + 1 < J:
                        to_channels(1, j + 1)
                    pe.wait_ge(s_xhs, b * (2 * J) + J + j + 1)
                    for k in range(CT):
                        t = CT * j + k
                        last = mm(ps[:, 2, E * t:E * t + E], xhT[:, P * t:P * t + P], rw[:, :], start=True, stop=True)
                last.then_inc(s_rl, 1)
                pe.wait_ge(s_g, b + 1)
                gate = psum4[:, 1:3, :].rearrange("p a b -> p (a b)")
                for k in range(J):
                    last = nc.tensor.transpose(ps[:, 3 + k // 4, P * (k % 4):P * (k % 4) + P],
                                               gate[:, P * k:P * k + P], ident)
                last.then_inc(s_gT, 1)
                pe.wait_ge(s_gTs, b + 1)
                for j in range(J):
                    if j >= 2:
                        pe.wait_ge(s_ebu, b * J + j - 1)
                    gT = (work[:, 1, :] if j < 4 else psum4[:, 0, :])[:, P * (j % 4):P * (j % 4) + P]
                    for k in range(CT):
                        last = mm(ps[:, 6 + j % 2, P * k:P * k + P], gT, eb[:, k, :],
                                  start=True, stop=True)
                    last.then_inc(s_eb, 1)
                    for k in range(CT):
                        t = CT * j + k
                        if t >= 3:
                            pe.wait_ge(s_yu, b * T + t - 2)
                            pe.wait_ge(s_ys, b * T + t - 2)
                        for half in range(2):
                            last = mm(ps[:, 2 * (t % 3) + half, :], xhT[:, P * t:P * t + P],
                                      ew[:, 4 * half:4 * half + 4, :], start=True, stop=True)
                        last.then_inc(s_y, 1)
                pe.wait_ge(s_y, b * T + T)
                pe.sem_inc(s_batch, 1)


_INS = ["x", "L0_conv_W1", "L0_conv_b1", "L0_conv_W2", "L0_conv_b2", "L0_conv_Wq", "L0_conv_bq", "L0_conv_Wk",
        "L0_conv_bk", "L0_conv_Wv", "L0_conv_bv", "L0_conv_W3", "L0_conv_b3", "L1_attn_W_qkv", "L1_attn_b_qkv",
        "L1_attn_W_proj", "L1_attn_b_proj", "L1_ffn_router_w", "L1_ffn_router_b", "L1_ffn_expert_w",
        "L1_ffn_expert_b"]


def kernel(**inputs):
    import numpy as np
    import concourse.bacc as bacc
    from concourse.bass_utils import run_bass_kernel_spmd

    nc = bacc.Bacc("TRN2", target_bir_lowering=False, num_devices=1)
    arrays, args = {}, {}
    for name in _INS:
        arrays[f"in_{name}"] = np.ascontiguousarray(inputs[name])
        args[name] = nc.dram_tensor(f"in_{name}", arrays[f"in_{name}"].shape, F32, kind="ExternalInput").ap()
    arrays["in_constants"] = constants()
    consts = nc.dram_tensor("in_constants", (P, C_COLS), F32, kind="ExternalInput").ap()
    out = nc.dram_tensor("out_0", (B, IMG, IMG, P), F32, kind="ExternalOutput").ap()
    conv_hybrid_kernel(nc, args, consts, out)
    r = run_bass_kernel_spmd(nc, [arrays], core_ids=[0])
    return r.results[0]["out_0"]
```
